# Optimizing a Trainium2 kernel written in Bass

```python
import numpy as np
import jax
import jax.numpy as jnp

def _softmax(x, axis=-1):
    return jax.nn.softmax(x, axis=axis)

def _gelu(x):
    return jax.nn.gelu(x, approximate=True)

def _silu(x):
    return jax.nn.silu(x)

def _sigmoid(x):
    return jax.nn.sigmoid(x)

def _layernorm(x, axis=-1, eps=1e-05):
    m = jnp.mean(x, axis=axis, keepdims=True)
    v = jnp.var(x, axis=axis, keepdims=True)
    return (x - m) / jnp.sqrt(v + eps)

def _scatter_add(tgt, idx, src, axis=0):
    return tgt.at[idx].add(src)

def _segment_sum(src, seg, n):
    return jax.ops.segment_sum(src, seg, n)
kernel_name = 'mk_gnn_resnorm_d1_gnn_r8_8d9e11'

def setup_inputs(seed: int=0):
    np.random.seed(seed)
    _w = jnp.asarray

    def _rec_inputs():
        import jax
        import jax.numpy as jnp
        _gk = jax.random.key(seed)
        x = -0.000202 + 1 * jax.random.normal(jax.random.fold_in(_gk, 1), (6250, 256), jnp.float32)
        src = jax.random.randint(jax.random.fold_in(_gk, 2), (200000,), 0, 6250, jnp.int32)
        dst = jax.random.randint(jax.random.fold_in(_gk, 3), (200000,), 0, 6250, jnp.int32)
        _o = jnp.argsort(dst, stable=True)
        src = src[_o]
        dst = dst[_o]
        return (x, src, dst)
    x, src, dst = _rec_inputs()

    def _L0_gnn_setup():
        import jax, jax.numpy as jnp
        import numpy as np
        N_NODES = 3125
        N_EDGES = 50000
        D = 256
        key = jax.random.key(seed)
        k1, k2, k3, k4, k5 = jax.random.split(key, 5)
        feat = jax.random.normal(k1, (N_NODES, D), dtype=jnp.float32)
        src = jax.random.randint(k2, (N_EDGES,), 0, N_NODES, dtype=jnp.int32)
        dst = jax.random.randint(k3, (N_EDGES,), 0, N_NODES, dtype=jnp.int32)
        a = float(np.sqrt(6.0 / (D + D)))
        W1 = jax.random.uniform(k4, (D, D), minval=-a, maxval=a, dtype=jnp.float32)
        W2 = jax.random.uniform(k5, (D, D), minval=-a, maxval=a, dtype=jnp.float32)
        b = jnp.zeros((D,), dtype=jnp.float32)
        return {'feat': feat, 'W1': W1, 'W2': W2, 'b': b, 'src': src, 'dst': dst}
    _L0_gnn_all = _L0_gnn_setup()
    _L0_gnn_in = {k: v for k, v in _L0_gnn_all.items() if k in ('W1', 'W2', 'b')}
    del _L0_gnn_all
    return {'x': x, 'src': src, 'dst': dst, 'L0_gnn_W1': _L0_gnn_in['W1'], 'L0_gnn_W2': _L0_gnn_in['W2'], 'L0_gnn_b': _L0_gnn_in['b']}

def reference(x, src, dst, L0_gnn_W1, L0_gnn_W2, L0_gnn_b):
    import jax
    import jax.numpy as jnp

    def _L0_gnn_ref(feat, W1, W2, b, src, dst):
        import jax, jax.numpy as jnp
        import numpy as np
        N_NODES = 3125
        N_EDGES = 50000
        D = 256
        n = feat.shape[0]
        ones = jnp.ones(src.shape[0], dtype=feat.dtype)
        out_deg = jnp.maximum(jax.ops.segment_sum(ones, src, num_segments=n), 1.0)
        in_cnt = jax.ops.segment_sum(ones, dst, num_segments=n)
        t1 = feat @ W1
        msg = t1[src] + feat[src] * feat[dst] @ W2
        scale = jnp.sqrt(out_deg[src]) * jnp.sqrt(out_deg[dst])
        msg = msg / scale[:, None]
        agg = jax.ops.segment_sum(msg, dst, num_segments=n)
        embed = jnp.where(in_cnt[:, None] > 0, t1 + agg, jnp.zeros_like(t1))
        embed = embed + b
        embed = jax.nn.leaky_relu(embed, negative_slope=0.01)
        norm = jnp.linalg.norm(embed, axis=1, keepdims=True)
        embed = embed / jnp.maximum(norm, 1e-12)
        return embed
    x = _layernorm(x + _L0_gnn_ref(x, L0_gnn_W1, L0_gnn_W2, L0_gnn_b, src, dst), axis=-1)
    return x

_drawn_inputs = setup_inputs


def setup_inputs(seed=0):
    import zlib

    import numpy as np

    out = dict(_drawn_inputs(seed))
    spreads = {'L0_gnn_b': (0.0, 0.8)}
    factors = {'L0_gnn_W2': 5.306}
    for name, (base, spread) in spreads.items():
        noise = np.random.default_rng([zlib.crc32(name.encode()), seed]).standard_normal(out[name].shape)
        drawn = base * np.exp(spread * noise) if base else spread * noise
        out[name] = jnp.asarray(drawn.astype(out[name].dtype))
    for name, factor in factors.items():
        out[name] = (out[name] * factor).astype(out[name].dtype)
    return out
```

```python
from contextlib import ExitStack

import concourse.bass as bass
from concourse import mybir

F32 = mybir.dt.float32
BF16 = mybir.dt.bfloat16
I32 = mybir.dt.int32
ALU = mybir.AluOpType
ACT = mybir.ActivationFunctionType
AX_X = mybir.AxisListType.X

P = 128
TILES = 8
GROUPS = 4
W = 48
LAG = 2
PAD_ID = 8191
CHUNKS_OF_X = 7


def build(nc, x, src, dst, w1, w2, bias, out):
    N, D = x.shape
    E = src.shape[0]
    H = D // P
    BLOCKS = -(-N // P)
    ROWS_LAST = N - (BLOCKS - 1) * P
    STEP_TILES = TILES * GROUPS
    STEPS = -(-E // (P * STEP_TILES))
    assert STEPS == BLOCKS
    TC = -(-(STEPS * STEP_TILES + TILES) // P)
    TT = TC * P
    TG = TT // TILES
    FULL_CHUNKS = E // (P * P)
    REST = E - FULL_CHUNKS * P * P
    REST_ROWS, REST_EDGES = divmod(REST, P)
    BC = BLOCKS // CHUNKS_OF_X

    y_dram = nc.dram_tensor("y_scaled", [BLOCKS * P, D], F32, kind="Internal").ap()

    ctx = ExitStack()
    with ctx:
        def sb(name, shape, dt):
            return ctx.enter_context(nc.sbuf_tensor(name, shape, dt))

        def ps(name, shape, dt=F32):
            return ctx.enter_context(nc.psum_tensor(name, shape, dt))

        def sem(name):
            return ctx.enter_context(nc.semaphore(name))

        ident = sb("ident", [P, P], F32)
        ones = sb("ones", [P, P], F32)
        iota_i = sb("iota_i", [P, P], I32)
        iota_f = sb("iota_f", [P, P], F32)
        iota_b = sb("iota_b", [P, P], BF16)
        w1_sb = sb("w1_sb", [P, H, D], F32)
        w2_sb = sb("w2_sb", [P, H, D], F32)
        bias_sb = sb("bias_sb", [P, D], F32)
        idx_tab = sb("idx_tab", [P, TT], I32)
        rel = sb("rel", [P, TT], F32)
        base_i = sb("base_i", [1, TG], I32)
        deg = sb("deg", [P, BLOCKS], F32)
        rs = sb("rs", [P, BLOCKS], F32)
        rtmp = sb("rtmp", [P, BLOCKS], F32)
        gT = sb("gT", [P, H, BLOCKS * P + W], F32)
        cnt = sb("cnt", [1, BLOCKS * P + W], F32)
        idx8 = sb("idx8", [P, GROUPS, TILES], I32)
        hot = sb("hot", [P, 2, TILES, W], F32)

        s_const = sem("s_const"); s_iota = sem("s_iota")
        s_w = sem("s_w"); s_edges = sem("s_edges"); s_x = sem("s_x")
        s_pad = sem("s_pad"); s_edgef = sem("s_edgef"); s_tr = sem("s_tr"); s_trc = sem("s_trc")
        s_tab = sem("s_tab"); s_basep = sem("s_basep"); s_setup = sem("s_setup")
        s_lohot = sem("s_lohot"); s_histdone = sem("s_histdone"); s_histadd = sem("s_histadd")
        s_deg = sem("s_deg"); s_sqrt = sem("s_sqrt"); s_r = sem("s_r")
        s_y = sem("s_y"); s_ystore = sem("s_ystore"); s_gzero = sem("s_gzero")
        s_idx = sem("s_idx"); s_rows = [sem(f"s_rows{q}") for q in range(GROUPS)]
        s_hot = sem("s_hot"); s_grp = sem("s_grp"); s_acc = sem("s_acc")
        s_xb = sem("s_xb"); s_xbT = sem("s_xbT"); s_xT = sem("s_xT"); s_gx = sem("s_gx")
        s_prod = sem("s_prod"); s_a = sem("s_a"); s_emb = sem("s_emb"); s_norm = sem("s_norm")
        s_var = sem("s_var"); s_std = sem("s_std"); s_o = sem("s_o"); s_out = sem("s_out")
        s_cntT = sem("s_cntT"); s_v = sem("s_v"); s_sq = sem("s_sq"); s_ysum = sem("s_ysum")

        ph1 = ExitStack()
        with ph1:
            def sb1(name, shape, dt):
                return ph1.enter_context(nc.sbuf_tensor(name, shape, dt))

            edge_i = sb1("edge_i", [P, 2, TC, P], I32)
            edge_f = sb1("edge_f", [P, 2, TC, P], F32)
            srcT = sb1("srcT", [P, TT], F32)
            srcT_i = edge_i[:, 0, :, :].rearrange("p c e -> p (c e)")
            bits = edge_f[:, :, :, :].bitcast(I32).rearrange("p k c e -> p k (c e)")
            lohi = sb1("lohi", [P, 2, TT], BF16)
            lo_hot = sb1("lo_hot", [P, 2, TILES, P], BF16)
            hi_hot = sb1("hi_hot", [P, 2, TILES, BLOCKS], BF16)
            xs = sb1("xs", [P, BLOCKS, D], F32)
            tr_ps = ph1.enter_context(nc.psum_tensor("tr_ps", [P, 2, 512], F32))
            base_ps = ph1.enter_context(nc.psum_tensor("base_ps", [P, 512], F32))
            hist_ps = ph1.enter_context(nc.psum_tensor("hist_ps", [P, 2, 512], F32))

            batches = [(s, c, min(4, TC - c)) for s in range(2) for c in range(0, TC, 4)]
            dstT = rel

            with nc.Block() as block:
                @block.sync
                def _(sp):
                    sp.wait_ge(s_pad, 1)
                    for k, e in enumerate((src, dst)):
                        sp.dma_start(edge_i[:, k, 0:FULL_CHUNKS, :],
                                     e[0:FULL_CHUNKS * P * P].rearrange("(c q e) -> q c e", q=P, e=P)
                                     ).then_inc(s_edges, 16)
                        at = FULL_CHUNKS * P * P
                        sp.dma_start(edge_i[0:REST_ROWS, k, FULL_CHUNKS, :],
                                     e[at:at + REST_ROWS * P].rearrange("(q e) -> q e", e=P)
                                     ).then_inc(s_edges, 16)
                        at += REST_ROWS * P
                        sp.dma_start(edge_i[REST_ROWS:REST_ROWS + 1, k, FULL_CHUNKS, 0:REST_EDGES],
                                     e[at:at + REST_EDGES].rearrange("(o e) -> o e", o=1)
                                     ).then_inc(s_edges, 16)
                    sp.dma_start(xs[:, 0:BLOCKS - 1, :],
                                 x[0:(BLOCKS - 1) * P, :].rearrange("(c p) d -> p c d", p=P)).then_inc(s_x, 16)
                    sp.dma_start(xs[0:ROWS_LAST, BLOCKS - 1, :], x[(BLOCKS - 1) * P:N, :]).then_inc(s_x, 16)
                    sp.dma_start(w1_sb[:, :, :], w1.rearrange("(h p) d -> p h d", p=P)).then_inc(s_w, 16)
                    sp.dma_start(w2_sb[:, :, :], w2.rearrange("(h p) d -> p h d", p=P)).then_inc(s_w, 16)
                    sp.dma_start(bias_sb[:, :], bias.rearrange("(o d) -> o d", o=1).to_broadcast([P, D])
                                 ).then_inc(s_w, 16)
                    for c in range(CHUNKS_OF_X):
                        sp.wait_ge(s_y, c + 1)
                        sp.dma_start(y_dram[c * BC * P:(c + 1) * BC * P, :].rearrange("(c p) d -> p c d", p=P),
                                     xs[:, c * BC:(c + 1) * BC, :]).then_inc(s_ystore, 16)
                    sp.wait_ge(s_ystore, 16 * CHUNKS_OF_X)
                    sp.wait_ge(s_w, 48)

                @block.gpsimd
                def _(pool):
                    for k in range(2):
                        last = nc.gpsimd.memset(edge_i[:, k, FULL_CHUNKS:TC, :], PAD_ID)
                    nc.gpsimd.memset(xs[:, BLOCKS - 1, :], 0.0)
                    nc.gpsimd.memset(ident[:, :], 0.0)
                    nc.gpsimd.memset(ones[:, :], 1.0)
                    nc.gpsimd.iota(iota_i[:, :], pattern=[[1, P]], base=0, channel_multiplier=0)
                    nc.gpsimd.drain().then_inc(s_pad, 1)
                    pool.wait_ge(s_pad, 1)
                    nc.gpsimd.affine_select(out=ident[:, :], in_=ident[:, :], compare_op=ALU.not_equal, fill=1.0,
                                            base=0, pattern=[[-1, P]], channel_multiplier=1).then_inc(s_const, 1)
                    nc.gpsimd.memset(gT[:, :, :], 0.0)
                    nc.gpsimd.memset(cnt[:, :], 0.0).then_inc(s_gzero, 1)

                @block.vector
                def _(dve):
                    n = [0]

                    def link(ins):
                        n[0] += 1
                        ins.then_inc(s_setup, 1)
                        dve.wait_ge(s_setup, n[0])

                    dve.wait_ge(s_pad, 1)
                    nc.vector.memset(deg[:, :], 0.0)
                    nc.vector.tensor_copy(iota_f[:, :], iota_i[:, :])
                    link(nc.vector.tensor_copy(iota_b[:, :], iota_i[:, :]))
                    dve.wait_ge(s_edges, 96)
                    nc.vector.tensor_copy(edge_f[:, 0, :, :], edge_i[:, 0, :, :]).then_inc(s_edgef, 1)
                    nc.vector.tensor_copy(edge_f[:, 1, :, :], edge_i[:, 1, :, :]).then_inc(s_edgef, 1)
                    for b, (k, c, m) in enumerate(batches):
                        dve.wait_ge(s_tr, b + 1)
                        nc.vector.tensor_copy((srcT, dstT)[k][:, c * P:(c + m) * P],
                                              tr_ps[:, b % 2, 0:m * P]).then_inc(s_trc, 1)
                    dve.wait_ge(s_trc, len(batches))
                    link(nc.vector.tensor_copy(srcT_i[:, :], srcT[:, :]))
                    nc.vector.tensor_single_scalar(bits[:, 0, :], srcT_i[:, :], P - 1, ALU.bitwise_and)
                    link(nc.vector.tensor_single_scalar(bits[:, 1, :], srcT_i[:, :], 7, ALU.arith_shift_right))
                    link(nc.vector.tensor_copy(lohi[:, :, :], bits[:, :, :]))
                    nc.vector.tensor_scalar(idx_tab[:, :], srcT[:, :], float(N - 1), None, ALU.min)
                    dve.wait_ge(s_basep, 1)
                    nc.vector.tensor_copy(base_i[0:1, :], base_ps[0:1, 0:TG])
                    nc.vector.tensor_tensor(rel[:, :].rearrange("p (g t) -> p g t", t=TILES),
                                            dstT[:, :].rearrange("p (g t) -> p g t", t=TILES),
                                            base_ps[:, 0:TG].unsqueeze(2).to_broadcast([P, TG, TILES]),
                                            ALU.subtract).then_inc(s_tab, 1)
                    def factor_hots(g, half):
                        dve.wait_ge(s_histdone, g + 1)
                        cols = bass.ds(g * TILES, TILES)
                        nc.vector.tensor_tensor(lo_hot[:, half, :, :],
                                                iota_b[:, :].unsqueeze(1).to_broadcast([P, TILES, P]),
                                                lohi[:, 0, cols].unsqueeze(2).to_broadcast([P, TILES, P]),
                                                ALU.is_equal)
                        nc.vector.tensor_tensor(hi_hot[:, half, :, :],
                                                iota_b[:, 0:BLOCKS].unsqueeze(1).to_broadcast([P, TILES, BLOCKS]),
                                                lohi[:, 1, cols].unsqueeze(2).to_broadcast([P, TILES, BLOCKS]),
                                                ALU.is_equal).then_inc(s_lohot, 1)

                    factor_hots(0, 0)
                    with nc.vector.Fori(0, STEPS) as j:
                        for q in range(GROUPS):
                            g = j * GROUPS + q
                            factor_hots(g + 1, (q + 1) % 2)
                            dve.wait_ge(s_histdone, g + 3)
                            nc.vector.tensor_tensor(deg[:, :], deg[:, :], hist_ps[:, q % 2, 0:BLOCKS],
                                                    ALU.add).then_inc(s_histadd, 1)
                            dve.wait_ge(s_histadd, g + 1)
                    link(nc.vector.tensor_scalar(deg[:, :], deg[:, :], 1.0, None, ALU.max))
                    nc.vector.engine_nop().then_inc(s_deg, 1)
                    dve.wait_ge(s_sqrt, 1)
                    link(nc.vector.reciprocal(rs[:, :], rtmp[:, :]))
                    link(nc.vector.tensor_tensor(rtmp[:, :], rs[:, :], rs[:, :], ALU.mult))
                    link(nc.vector.tensor_tensor(rtmp[:, :], rtmp[:, :], deg[:, :], ALU.mult))
                    link(nc.vector.tensor_scalar(rtmp[:, :], rtmp[:, :], -0.5, 1.5, ALU.mult, ALU.add))
                    link(nc.vector.tensor_tensor(rs[:, :], rs[:, :], rtmp[:, :], ALU.mult))
                    dve.wait_ge(s_x, 32)
                    for c in range(CHUNKS_OF_X):
                        part = xs[:, c * BC:(c + 1) * BC, :]
                        nc.vector.tensor_tensor(part, part,
                                                rs[:, c * BC:(c + 1) * BC].unsqueeze(2).to_broadcast([P, BC, D]),
                                                ALU.mult).then_inc(s_y, 1)

                @block.scalar
                def _(act):
                    act.wait_ge(s_deg, 1)
                    nc.scalar.activation(rtmp[:, :], deg[:, :], ACT.Sqrt).then_inc(s_sqrt, 1)

                @block.tensor
                def _(pe):
                    pe.wait_ge(s_const, 1)
                    for b, (k, c, m) in enumerate(batches):
                        pe.wait_ge(s_edgef, k + 1)
                        if b >= 2:
                            pe.wait_ge(s_trc, b - 1)
                        for i in range(m):
                            last = nc.tensor.transpose(tr_ps[:, b % 2, i * P:(i + 1) * P],
                                                       edge_f[:, k, c + i, :], ident[:, :])
                        last.then_inc(s_tr, 1)
                    pe.wait_ge(s_trc, len(batches))
                    nc.tensor.matmul(base_ps[:, 0:TG], ones[0:1, :], dstT[0:1, 0:TT:TILES],
                                     start=True, stop=True).then_inc(s_basep, 1)
                    nc.tensor.sem_inc(s_histdone, 2)
                    with nc.tensor.Fori(0, STEPS) as j:
                        for q in range(GROUPS):
                            g = j * GROUPS + q
                            pe.wait_ge(s_lohot, g + 1)
                            for t in range(TILES):
                                last = nc.tensor.matmul(hist_ps[:, q % 2, 0:BLOCKS], lo_hot[:, q % 2, t, :],
                                                        hi_hot[:, q % 2, t, :], start=(t == 0), stop=(t == TILES - 1))
                            last.then_inc(s_histdone, 1)

        rows = sb("rows", [P, GROUPS, TILES, D], F32)
        xb = sb("xb", [P, 2, D], F32)
        xT = sb("xT", [P, H, P], F32)
        gx = sb("gx", [P, H, P], F32)
        gb = sb("gb", [P, H, P], F32)
        cb = sb("cb", [1, P], F32)
        a_sb = sb("a_sb", [P, D], F32)
        emb = sb("emb", [P, D], F32)
        sq = sb("sq", [P, D], F32)
        ysum = sb("ysum", [P, D], F32)
        o_sb = sb("o_sb", [P, D], F32)
        has = sb("has", [P, 1], F32)
        ss = sb("ss", [P, 1], F32)
        nrm = sb("nrm", [P, 1], F32)
        inv = sb("inv", [P, 1], F32)
        stats = sb("stats", [P, 6], F32)
        mv = sb("mv", [P, 2], F32)
        veps = sb("veps", [P, 1], F32)
        std = sb("std", [P, 1], F32)
        rstd = sb("rstd", [P, 1], F32)
        grp_ps = ps("grp_ps", [P, 2, 512])
        xT_ps = ps("xT_ps", [P, 512])
        a_ps = ps("a_ps", [P, 512])
        b_ps = ps("b_ps", [P, 512])

        GROUP_SUM = GROUPS * STEPS
        CW = H * W

        def block_rows(b):
            return ROWS_LAST if isinstance(b, int) and b == BLOCKS - 1 else P

        with nc.Block() as block:
            @block.sync
            def _(sp):
                def load_block(b):
                    n = block_rows(b)
                    sp.dma_start(xb[0:n, 0, :], x[bass.ds(b * P, n), :]).then_inc(s_xb, 16)

                def store_block(b):
                    n = block_rows(b)
                    sp.wait_ge(s_o, b + 1)
                    sp.dma_start(out[bass.ds(b * P, n), :], o_sb[0:n, :]).then_inc(s_out, 16)
                    sp.wait_ge(s_out, b * 16 + 16)

                load_block(0)
                with nc.sync.Fori(0, BLOCKS - 2) as b:
                    store_block(b)
                    load_block(b + 1)
                store_block(BLOCKS - 2)
                load_block(BLOCKS - 1)
                store_block(BLOCKS - 1)

            @block.gpsimd
            def _(pool):
                with nc.gpsimd.Fori(0, STEPS) as j:
                    for q in range(GROUPS):
                        pool.wait_ge(s_idx, j * GROUPS + (q + 1))
                        nc.gpsimd.nop(nofuse=True)
                        pool.wait_ge(s_grp, j * GROUPS + (q + 1))
                        nc.gpsimd.nop(nofuse=True)
                        for t in range(TILES):
                            nc.gpsimd.indirect_dma_start(
                                out=rows[:, q, t, :], out_offset=None, in_=y_dram[:, :],
                                in_offset=bass.IndirectOffsetOnAxis(ap=idx8[:, q, t:t + 1], axis=0)
                            ).then_inc(s_rows[q], 16)

            @block.scalar
            def _(act):
                def copy_idx(j, q):
                    nc.scalar.copy(idx8[:, q, :], idx_tab[:, bass.ds((j * GROUPS + q) * TILES, TILES)]
                                   ).then_inc(s_idx, 1)

                def next_idx(j, q):
                    act.wait_ge(s_rows[q], j * (16 * TILES) + 16 * TILES)
                    copy_idx(j + 1, q)

                def xT_copy(b):
                    n = block_rows(b)
                    act.wait_ge(s_xbT, b + 1)
                    nc.scalar.copy(xT[:, :, 0:n], xT_ps[:, 0:H * P].rearrange("p (h n) -> p h n", h=H)[:, :, 0:n]
                                   ).then_inc(s_xT, 1)

                def a_copy(b):
                    n = block_rows(b)
                    act.wait_ge(s_prod, b + 1)
                    nc.scalar.copy(a_sb[0:n, :], a_ps[0:n, 0:D]).then_inc(s_a, 1)

                def row_norm(b):
                    n = block_rows(b)
                    act.wait_ge(s_emb, b + 1)
                    nc.scalar.activation(sq[0:n, :], emb[0:n, :], ACT.Square, accum_out=ss[0:n, :]).then_inc(s_sq, 1)
                    act.wait_ge(s_sq, b + 1)
                    nc.scalar.activation(nrm[0:n, :], ss[0:n, :], ACT.Sqrt).then_inc(s_norm, 1)

                def row_std(b):
                    n = block_rows(b)
                    act.wait_ge(s_var, b + 1)
                    nc.scalar.activation(std[0:n, :], veps[0:n, :], ACT.Sqrt).then_inc(s_std, 1)

                def finish(b):
                    xT_copy(b)
                    a_copy(b)
                    row_norm(b)
                    row_std(b)

                for q in range(GROUPS):
                    copy_idx(0, q)
                with nc.scalar.Fori(0, LAG) as j:
                    for q in range(GROUPS):
                        next_idx(j, q)
                with nc.scalar.Fori(LAG, STEPS - 1) as j:
                    b = j - LAG
                    next_idx(j, 0)
                    xT_copy(b)
                    next_idx(j, 1)
                    a_copy(b)
                    next_idx(j, 2)
                    row_norm(b)
                    next_idx(j, 3)
                    row_std(b)
                for b in range(STEPS - 1 - LAG, BLOCKS):
                    finish(b)

            @block.tensor
            def _(pe):
                def group(j, q):
                    g = j * GROUPS + q
                    pe.wait_ge(s_rows[q], j * (16 * TILES) + 16 * TILES)
                    pe.wait_ge(s_hot, g + 1)
                    pe.wait_ge(s_acc, g + 1)
                    for h in range(H):
                        for t in range(TILES):
                            nc.tensor.matmul(grp_ps[:, q % 2, h * W:(h + 1) * W], rows[:, q, t, h * P:(h + 1) * P],
                                             hot[:, q % 2, t, :], start=(t == 0), stop=(t == TILES - 1))
                    for t in range(TILES):
                        last = nc.tensor.matmul(grp_ps[0:1, q % 2, CW:CW + W], ones[:, 0:1],
                                                hot[:, q % 2, t, :], start=(t == 0), stop=(t == TILES - 1))
                    last.then_inc(s_grp, 1)

                def transpose_x(b):
                    n = block_rows(b)
                    pe.wait_ge(s_xb, b * 16 + 16)
                    for h in range(H):
                        last = nc.tensor.transpose(xT_ps[:, h * P:h * P + n], xb[0:n, 0, h * P:(h + 1) * P],
                                                   ident[0:n, 0:n])
                    last.then_inc(s_xbT, 1)

                def products(b):
                    n = block_rows(b)
                    pe.wait_ge(s_xT, b + 1)
                    pe.wait_ge(s_gx, b + 1)
                    for h in range(H):
                        nc.tensor.matmul(a_ps[0:n, 0:D], xT[:, h, 0:n], w1_sb[:, h, :],
                                         start=(h == 0), stop=(h == H - 1))
                    nc.tensor.matmul(a_ps[0:n, D:D + 1], cb[0:1, 0:n], ones[0:1, 0:1],
                                     start=True, stop=True)
                    for h in range(H):
                        nc.tensor.matmul(b_ps[0:n, 0:D], gb[:, h, 0:n], w1_sb[:, h, :],
                                         start=(h == 0), stop=False)
                    for h in range(H):
                        last = nc.tensor.matmul(b_ps[0:n, 0:D], gx[:, h, 0:n], w2_sb[:, h, :],
                                                start=False, stop=(h == H - 1))
                    last.then_inc(s_prod, 1)

                nc.tensor.sem_inc(s_grp, GROUPS)
                with nc.tensor.Fori(0, LAG) as j:
                    for q in range(GROUPS):
                        group(j, q)
                with nc.tensor.Fori(LAG, STEPS) as j:
                    b = j - LAG
                    group(j, 0)
                    transpose_x(b)
                    group(j, 1)
                    products(b)
                    group(j, 2)
                    group(j, 3)
                for b in range(STEPS - LAG, BLOCKS):
                    transpose_x(b)
                    products(b)

            @block.vector
            def _(dve):
                def one_hots(j, q):
                    g = j * GROUPS + q
                    dve.wait_ge(s_grp, g + GROUPS - 1)
                    nc.vector.tensor_tensor(hot[:, q % 2, :, :],
                                            iota_f[:, 0:W].unsqueeze(1).to_broadcast([P, TILES, W]),
                                            rel[:, bass.ds(g * TILES, TILES)].unsqueeze(2).to_broadcast([P, TILES, W]),
                                            ALU.is_equal).then_inc(s_hot, 1)

                def accumulate(j, q):
                    g = j * GROUPS + q
                    base = nc.vector.value_load(base_i[0:1, bass.ds(g, 1)], min_val=0, max_val=N - 1)
                    dve.wait_ge(s_grp, g + GROUPS + 1)
                    at = gT[:, :, bass.ds(base, W)]
                    nc.vector.tensor_tensor(at, at, grp_ps[:, q % 2, 0:CW].rearrange("p (h w) -> p h w", h=H), ALU.add)
                    at = cnt[0:1, bass.ds(base, W)]
                    nc.vector.tensor_tensor(at, at, grp_ps[0:1, q % 2, CW:CW + W], ALU.add).then_inc(s_acc, 1)
                    dve.wait_ge(s_acc, g + 3)

                def times_x(b):
                    n = block_rows(b)
                    nc.vector.tensor_copy(gb[:, :, 0:n], gT[:, :, bass.ds(b * P, n)])
                    nc.vector.tensor_copy(cb[0:1, 0:n], cnt[0:1, bass.ds(b * P, n)])
                    dve.wait_ge(s_xT, b + 1)
                    nc.vector.tensor_tensor(gx[:, :, 0:n], gT[:, :, bass.ds(b * P, n)], xT[:, :, 0:n],
                                            ALU.mult).then_inc(s_gx, 1)

                LINKS = 10

                def embed(b):
                    n = block_rows(b)
                    dve.wait_ge(s_a, b + 1)
                    nc.vector.tensor_scalar(has[0:n, :], a_ps[0:n, D:D + 1], 0.0, None, ALU.is_gt)
                    nc.vector.scalar_tensor_tensor(out=emb[0:n, :], in0=b_ps[0:n, 0:D], scalar=rs[0:n, bass.ds(b, 1)],
                                                   in1=a_sb[0:n, :], op0=ALU.mult, op1=ALU.add).then_inc(s_v, 1)
                    dve.wait_ge(s_v, b * LINKS + 1)
                    nc.vector.scalar_tensor_tensor(out=emb[0:n, :], in0=emb[0:n, :], scalar=has[0:n, :],
                                                   in1=bias_sb[0:n, :], op0=ALU.mult, op1=ALU.add).then_inc(s_v, 1)
                    dve.wait_ge(s_v, b * LINKS + 2)
                    nc.vector.scalar_tensor_tensor(out=emb[0:n, :], in0=emb[0:n, :], scalar=0.01,
                                                   in1=emb[0:n, :], op0=ALU.mult, op1=ALU.max).then_inc(s_emb, 1)

                def normalize(b):
                    n = block_rows(b)
                    dve.wait_ge(s_norm, b + 1)
                    nc.vector.tensor_scalar(nrm[0:n, :], nrm[0:n, :], 1e-12, None, ALU.max).then_inc(s_v, 1)
                    dve.wait_ge(s_v, b * LINKS + 3)
                    nc.vector.reciprocal(inv[0:n, :], nrm[0:n, :]).then_inc(s_v, 1)
                    dve.wait_ge(s_v, b * LINKS + 4)
                    nc.vector.scalar_tensor_tensor(out=ysum[0:n, :], in0=emb[0:n, :], scalar=inv[0:n, :],
                                                   in1=xb[0:n, 0, :], op0=ALU.mult, op1=ALU.add).then_inc(s_v, 1)
                    dve.wait_ge(s_v, b * LINKS + 5)
                    nc.vector.bn_stats(stats[0:n, :], ysum[0:n, :]).then_inc(s_v, 1)
                    dve.wait_ge(s_v, b * LINKS + 6)
                    nc.vector.nop(nofuse=True)
                    nc.vector.bn_aggr(mv[0:n, :], stats[0:n, :]).then_inc(s_v, 1)
                    dve.wait_ge(s_v, b * LINKS + 7)
                    nc.vector.tensor_scalar(veps[0:n, :], mv[0:n, 1:2], 1e-5, None, ALU.add).then_inc(s_var, 1)
                    dve.wait_ge(s_std, b + 1)
                    nc.vector.reciprocal(rstd[0:n, :], std[0:n, :]).then_inc(s_v, 3)
                    dve.wait_ge(s_v, b * LINKS + 10)
                    nc.vector.tensor_scalar(o_sb[0:n, :], ysum[0:n, :], mv[0:n, 0:1], rstd[0:n, :],
                                            ALU.subtract, ALU.mult).then_inc(s_o, 1)

                nc.vector.sem_inc(s_acc, 2)
                one_hots(0, 0)
                with nc.vector.Fori(0, LAG) as j:
                    for q in range(GROUPS):
                        one_hots(j, q + 1)
                        accumulate(j, q)
                with nc.vector.Fori(LAG, STEPS) as j:
                    b = j - LAG
                    one_hots(j, 1)
                    accumulate(j, 0)
                    times_x(b)
                    one_hots(j, 2)
                    accumulate(j, 1)
                    one_hots(j, 3)
                    accumulate(j, 2)
                    embed(b)
                    one_hots(j, 4)
                    accumulate(j, 3)
                    normalize(b)
                for b in range(STEPS - LAG, BLOCKS):
                    times_x(b)
                    embed(b)
                    normalize(b)


_INS = ['x', 'src', 'dst', 'L0_gnn_W1', 'L0_gnn_W2', 'L0_gnn_b']


def kernel(**inputs):
    import numpy as _np
    import concourse.bacc as _bacc
    from concourse import mybir as _mybir
    from concourse.bass_utils import run_bass_kernel_spmd as _run

    nc = _bacc.Bacc("TRN2", target_bir_lowering=False, num_devices=1)
    arrays, args = {}, []
    for name in _INS:
        a = _np.ascontiguousarray(inputs[name])
        arrays[f"in_{name}_dram"] = a
        args.append(nc.dram_tensor(f"in_{name}_dram", a.shape, _mybir.dt.from_np(a.dtype), kind="ExternalInput").ap())
    shape = tuple(inputs['x'].shape)
    args.append(nc.dram_tensor("out_0_dram", shape, _mybir.dt.float32, kind="ExternalOutput").ap())
    build(nc, *args)
    r = _run(nc, [arrays], core_ids=[0])
    return r.results[0]["out_0_dram"]
```

```python
from contextlib import ExitStack

import concourse.bass as bass
from concourse import mybir

F32 = mybir.dt.float32
BF16 = mybir.dt.bfloat16
I32 = mybir.dt.int32
U16 = mybir.dt.uint16
F16 = mybir.dt.float16
ALU = mybir.AluOpType
ACT = mybir.ActivationFunctionType
AX_X = mybir.AxisListType.X

P = 128
TILES = 8
RING = 4
QUARTERS = 4
W = 48
NEAR = 4
LAG = 2
GATHER_BLOCKS = 25
WN = 8
KEY_RING = 4
WT = 3
EROW = 32
PAD_ID = 8191
PARTS = 3
X_CHUNKS = 7
HT = 16
UNROLL = 14
FIRST_TURNS = 4
HIGH_ON_ACT = (0, 3, 6)
LOW_ON_DVE = ()
SPAN = 7
BATCH = 4
SLOTS = 8


def build(nc, x, src, dst, w1, w2, bias, out):
    N, D = x.shape
    E = src.shape[0]
    H = D // P
    BLOCKS = -(-N // P)
    BG = GATHER_BLOCKS
    BD = BLOCKS - BG
    ROWS_LAST = N - (BLOCKS - 1) * P
    HIST_GROUPS = -(-E // (P * HT))
    GROUPS = BG * QUARTERS + 1
    TC = -(-HIST_GROUPS * HT // P)
    TT = TC * P
    GT = -(-(GROUPS + 1) // QUARTERS) * QUARTERS * TILES
    FULL_CHUNKS = E // (P * P)
    REST_ROWS, REST_EDGES = divmod(E - FULL_CHUNKS * P * P, P)
    BC = BLOCKS // X_CHUNKS
    WB = P // WN
    WQ = WB // QUARTERS
    SETS = BD * WB // P
    WE = WT * P
    WROWS = WE // EROW
    ND0 = BG * P
    KEYS = WN * BLOCKS
    assert BD * WB == SETS * P and E % EROW == 0
    ROW_CHUNKS = TC * P // EROW
    WINDOWS = BD * WB
    TAKEN = GROUPS * TILES + SETS * WE + GROUPS

    y_dram = nc.dram_tensor("y_parts", [BLOCKS * P, PARTS * D], BF16, kind="Internal").ap()

    ctx = ExitStack()
    with ctx:
        def sb(name, shape, dt):
            return ctx.enter_context(nc.sbuf_tensor(name, shape, dt))

        def sem(name):
            return ctx.enter_context(nc.semaphore(name))

        ident = sb("ident", [P, P], F32)
        ones = sb("ones", [P, P], F32)
        ones_b = sb("ones_b", [P, 1], BF16)
        iota_f = sb("iota_f", [P, W], F32)
        iota_h = sb("iota_h", [P, KEYS], F16)
        w1_sb = sb("w1_sb", [P, H, D], F32)
        w2_sb = sb("w2_sb", [P, H, D], F32)
        bias_sb = sb("bias_sb", [P, D], F32)
        idx_tab = sb("idx_tab", [P, GT], U16)
        rel = sb("rel", [P, GT], F16)
        base_i = sb("base_i", [1, GT // TILES], I32)
        key_tab = sb("key_tab", [P, BD * WB * WT], F16)
        lo_tab = sb("lo_tab", [P, (BD * WB + 2 * WQ) * WT], F16)
        rs = sb("rs", [P, BLOCKS], F32)
        yp = sb("yp", [P, BLOCKS, PARTS, D], BF16)
        general = sb("general", [1, 1], I32)

        s_pad = sem("s_pad"); s_const = sem("s_const"); s_w = sem("s_w"); s_edges = [sem("s_edges_src"), sem("s_edges_dst")]
        s_x = sem("s_x"); s_edgef = sem("s_edgef"); s_tr = sem("s_tr"); s_trc = sem("s_trc")
        s_basep = sem("s_basep"); s_setup = sem("s_setup"); s_bcast = sem("s_bcast")
        s_widx = sem("s_widx"); s_wrow = sem("s_wrow"); s_wkey = sem("s_wkey")
        s_wtr = sem("s_wtr"); s_wtc = sem("s_wtc"); s_hot1 = sem("s_hot1")
        s_hist = sem("s_hist"); s_histall = sem("s_histall"); s_deg = sem("s_deg"); s_sqrt = sem("s_sqrt")
        s_hi = sem("s_hi"); s_r1 = sem("s_r1"); s_mid = sem("s_mid"); s_lo3 = sem("s_lo3")
        s_hi_act = sem("s_hi_act"); s_lo_dve = sem("s_lo_dve"); s_rs = sem("s_rs"); s_iotax = sem("s_iotax")
        s_edgef_src = sem("s_edgef_src"); s_below = sem("s_below")
        s_ystore = sem("s_ystore"); s_wpad = sem("s_wpad")
        s_near1 = sem("s_near1"); s_rel = sem("s_rel"); s_mask = sem("s_mask"); s_masked = sem("s_masked")
        s_total = sem("s_total"); s_flag = sem("s_flag")

        ph1 = ExitStack()
        with ph1:
            def sb1(name, shape, dt):
                return ph1.enter_context(nc.sbuf_tensor(name, shape, dt))

            iota_i = sb1("iota_i", [P, KEYS], I32)
            edge_i = sb1("edge_i", [P, 2, TC, P], I32)
            edge_f = sb1("edge_f", [P, 2, TC, P], F32)
            srcT = sb1("srcT", [P, TT], F32)
            dstT = sb1("dstT", [P, TT], F32)
            srcT_i = edge_i[:, 0, :, :].rearrange("p c e -> p (c e)")
            bits = edge_f[:, :, :, :].bitcast(I32).rearrange("p k c e -> p k (c e)")
            lohi = sb1("lohi", [P, 2, TT], BF16)
            iota_b = sb1("iota_b", [P, P], BF16)
            iota_x = sb1("iota_x", [P, P, HT], BF16)
            lo_hot1 = sb1("lo_hot1", [P, 2, P, HT], BF16)
            hi_hot1 = sb1("hi_hot1", [P, 2, BLOCKS, HT], BF16)
            zeros_b = sb1("zeros_b", [P, P], BF16)
            xs = sb1("xs", [P, BLOCKS, D], F32)
            deg = sb1("deg", [P, BLOCKS], F32)
            rtmp = sb1("rtmp", [P, BLOCKS], F32)
            thr_i = sb1("thr_i", [P, SETS], I32)
            thr = sb1("thr", [P, SETS], F32)
            held_i = sb1("held_i", [1, GT // TILES], I32)
            held = sb1("held", [1, GT // TILES], F32)
            near = sb1("near", [1, GT // TILES], F32)
            start_i = sb1("start_i", [P, WINDOWS], I32)
            start_h = sb1("start_h", [P, WINDOWS], F16)
            first = sb1("first", [P, SETS], F32)
            widx = sb1("widx", [P, SETS, WROWS], I32)
            in_reach = sb1("in_reach", [1, GROUPS], F32)
            total = sb1("total", [1, 1], F32)
            words = yp[:, :, :, :].rearrange("p b k d -> p (b k d)").bitcast(I32)
            WWORDS = 2 * SETS * WE
            wedge, wbits, wkey = (words[:, i * WWORDS:(i + 1) * WWORDS].rearrange("p (k s e) -> p k s e", k=2, s=SETS)
                                  for i in range(3))
            wkey = wkey.bitcast(F32)
            free = words[:, 3 * WWORDS:].bitcast(F32)
            in_group = free[:, 0:GROUPS * TILES]
            in_window = free[:, GROUPS * TILES:GROUPS * TILES + SETS * WE]
            taken = free[:, GROUPS * TILES + SETS * WE:].bitcast(BF16)[:, 0:TAKEN]
            starts_below = free[:, 0:ROW_CHUNKS * WINDOWS // 2].bitcast(BF16).rearrange("p (c w) -> p c w", w=WINDOWS)

            def ps1(name, shape):
                return ph1.enter_context(nc.psum_tensor(name, shape, F32))

            tr_ps = ps1("tr_ps", [P, 2, 512])
            base_ps = ps1("base_ps", [P, 512])
            hist_ps = ps1("hist_ps", [P, 512])
            below_ps = ps1("below_ps", [P, 512])
            wt_ps = ps1("wt_ps", [P, 2, 512])
            total_ps = base_ps

            batches = [(s, c, min(4, TC - c)) for s in (1, 0) for c in range(0, TC, 4)]
            DST_BATCHES = len(batches) // 2
            assert HIST_GROUPS % UNROLL == 0 and UNROLL % 2 == 0

            with nc.Block() as block:
                @block.sync
                def _(sp):
                    sp.wait_ge(s_pad, 1)
                    for k, e in ((1, dst), (0, src)):
                        sp.dma_start(edge_i[:, k, 0:FULL_CHUNKS, :],
                                     e[0:FULL_CHUNKS * P * P].rearrange("(c q e) -> q c e", q=P, e=P)
                                     ).then_inc(s_edges[k], 16)
                        at = FULL_CHUNKS * P * P
                        sp.dma_start(edge_i[0:REST_ROWS, k, FULL_CHUNKS, :],
                                     e[at:at + REST_ROWS * P].rearrange("(q e) -> q e", e=P)
                                     ).then_inc(s_edges[k], 16)
                        at += REST_ROWS * P
                        sp.dma_start(edge_i[REST_ROWS:REST_ROWS + 1, k, FULL_CHUNKS, 0:REST_EDGES],
                                     e[at:at + REST_EDGES].rearrange("(o e) -> o e", o=1)
                                     ).then_inc(s_edges[k], 16)
                    sp.dma_start(xs[:, 0:BLOCKS - 1, :],
                                 x[0:(BLOCKS - 1) * P, :].rearrange("(c p) d -> p c d", p=P)).then_inc(s_x, 16)
                    sp.dma_start(xs[0:ROWS_LAST, BLOCKS - 1, :], x[(BLOCKS - 1) * P:N, :]).then_inc(s_x, 16)
                    sp.dma_start(w1_sb[:, :, :], w1.rearrange("(h p) d -> p h d", p=P)).then_inc(s_w, 16)
                    sp.dma_start(w2_sb[:, :, :], w2.rearrange("(h p) d -> p h d", p=P)).then_inc(s_w, 16)
                    sp.dma_start(bias_sb[:, :], bias.rearrange("(o d) -> o d", o=1).to_broadcast([P, D])
                                 ).then_inc(s_w, 16)
                    for c in range(X_CHUNKS):
                        if c + 1 in LOW_ON_DVE:
                            sp.wait_ge(s_lo_dve, sum(i <= c + 1 for i in LOW_ON_DVE))
                        else:
                            sp.wait_ge(s_lo3, sum(i + 1 not in LOW_ON_DVE for i in range(c + 1)))
                        sp.dma_start(y_dram[c * BC * P:(c + 1) * BC * P, :].rearrange("(c p) d -> p c d", p=P),
                                     yp[:, c * BC:(c + 1) * BC, :, :].rearrange("p c k d -> p c (k d)")
                                     ).then_inc(s_ystore, 16)
                    sp.wait_ge(s_w, 48)

                @block.gpsimd
                def _(pool):
                    for k in range(2):
                        nc.gpsimd.memset(edge_i[:, k, FULL_CHUNKS:TC, :], PAD_ID)
                    nc.gpsimd.memset(xs[:, BLOCKS - 1, :], 0.0)
                    nc.gpsimd.memset(ident[:, :], 0.0)
                    nc.gpsimd.memset(ones[:, :], 1.0)
                    nc.gpsimd.memset(ones_b[:, :], 1.0)
                    nc.gpsimd.memset(zeros_b[:, :], 0.0)
                    nc.gpsimd.iota(thr_i[:, :], pattern=[[WN * P, SETS]], base=ND0, channel_multiplier=WN)
                    nc.gpsimd.iota(held_i[0:1, :], pattern=[[P, GT // TILES // QUARTERS], [0, QUARTERS]], base=-LAG * P,
                                   channel_multiplier=0)
                    nc.gpsimd.iota(iota_i[:, :], pattern=[[1, KEYS]], base=0, channel_multiplier=0)
                    nc.gpsimd.iota(start_i[:, :], pattern=[[WN, WINDOWS]], base=ND0, channel_multiplier=0)
                    nc.gpsimd.drain().then_inc(s_pad, 1)
                    pool.wait_ge(s_pad, 1)
                    nc.gpsimd.affine_select(out=ident[:, :], in_=ident[:, :], compare_op=ALU.not_equal, fill=1.0,
                                            base=0, pattern=[[-1, P]], channel_multiplier=1).then_inc(s_const, 1)
                    nc.gpsimd.memset(wedge[:, :, :, :], PAD_ID).then_inc(s_wpad, 1)
                    pool.wait_ge(s_wpad, 1)
                    pool.wait_ge(s_widx, 1)
                    for s in range(SETS):
                        for r in range(WROWS):
                            for k, e in enumerate((src, dst)):
                                nc.gpsimd.indirect_dma_start(
                                    out=wedge[:, k, s, r * EROW:(r + 1) * EROW], out_offset=None,
                                    in_=e.rearrange("(r e) -> r e", e=EROW),
                                    in_offset=bass.IndirectOffsetOnAxis(ap=widx[:, s, r:r + 1], axis=0),
                                    bounds_check=E // EROW - 1, oob_is_err=False).then_inc(s_wrow, 16)
                    GE = GROUPS * TILES
                    m = [0]

                    def link(ins):
                        m[0] += 1
                        ins.then_inc(s_mask, 1)
                        pool.wait_ge(s_mask, m[0])

                    def within(mask, values, low, high):
                        link(nc.gpsimd.tensor_scalar(mask, values, low, high, ALU.max, ALU.min))
                        link(nc.gpsimd.tensor_tensor(mask, mask, values, ALU.subtract))
                        link(nc.gpsimd.tensor_scalar(mask, mask, 0.0, None, ALU.is_equal))

                    pool.wait_ge(s_near1, 1)
                    within(in_reach[:, :], near[0:1, 0:GROUPS], float(P), float(NEAR * P))
                    pool.wait_ge(s_rel, 1)
                    within(in_group[:, :], rel[:, 0:GE], 0.0, float(W - 1))
                    pool.wait_ge(s_wkey, 1)
                    within(in_window[:, :], wkey[:, 0, :, :].rearrange("p s e -> p (s e)"), 0.0, float(KEYS - 1))
                    nc.gpsimd.memset(taken[:, GE + SETS * WE:], 0.0)
                    link(nc.gpsimd.tensor_copy(taken[:, GE:GE + SETS * WE], in_window[:, :]))
                    in_part = in_window[:, 0:GE]
                    link(nc.gpsimd.tensor_scalar(in_part, dstT[:, 0:GE], float(ND0), None, ALU.is_lt))
                    nc.gpsimd.tensor_tensor(taken[:, 0:GE], in_part, in_group[:, :], ALU.mult)
                    nc.gpsimd.tensor_copy(taken[0:1, GE + SETS * WE:], in_reach[:, :]).then_inc(s_masked, 1)
                    for c in range(X_CHUNKS):
                        if c + 1 not in LOW_ON_DVE:
                            pool.wait_ge(s_mid, c + 1)
                            b = slice(c * BC, (c + 1) * BC)
                            nc.gpsimd.tensor_tensor(yp[:, b, 2, :], xs[:, b, :], yp[:, b, 1, :],
                                                    ALU.subtract).then_inc(s_lo3, 1)

                @block.vector
                def _(dve):
                    n = [0]

                    def link(ins):
                        n[0] += 1
                        ins.then_inc(s_setup, 1)
                        dve.wait_ge(s_setup, n[0])

                    dve.wait_ge(s_pad, 1)
                    nc.vector.memset(lo_tab[:, BD * WB * WT:], 0.0)
                    nc.vector.tensor_copy(iota_f[:, :], iota_i[:, 0:W])
                    nc.vector.tensor_copy(thr[:, :], thr_i[:, :])
                    nc.vector.tensor_copy(held[0:1, :], held_i[0:1, :])
                    nc.vector.tensor_copy(iota_h[:, :], iota_i[:, :])
                    nc.vector.tensor_copy(start_h[:, :], start_i[:, :])
                    link(nc.vector.tensor_copy(iota_b[:, :], iota_i[:, 0:P]))
                    dve.wait_ge(s_edges[1], 48)
                    nc.vector.tensor_copy(edge_f[:, 1, :, :], edge_i[:, 1, :, :]).then_inc(s_edgef, 1)
                    dve.wait_ge(s_edgef, 1)
                    row_starts = edge_f[:, 1, :, :].rearrange("p c (r e) -> p (c r) e", e=EROW)
                    for c in range(ROW_CHUNKS):
                        nc.vector.tensor_scalar(starts_below[:, c, :], start_h[:, :], row_starts[:, c, 0:1], None,
                                                ALU.is_gt).then_inc(s_below, 1)
                    dve.wait_ge(s_bcast, 1)
                    link(nc.vector.tensor_scalar(first[:, :], below_ps[:, 0:SETS], -1.0, 0.0, ALU.add, ALU.max))
                    nc.vector.tensor_tensor(widx[:, :, :], first[:, :].unsqueeze(2).to_broadcast([P, SETS, WROWS]),
                                            iota_f[:, 0:WROWS].unsqueeze(1).to_broadcast([P, SETS, WROWS]),
                                            ALU.add).then_inc(s_widx, 1)
                    dve.wait_ge(s_trc, len(batches))
                    link(nc.vector.tensor_copy(srcT_i[:, :], srcT[:, :]))
                    nc.vector.tensor_single_scalar(bits[:, 0, :], srcT_i[:, :], P - 1, ALU.bitwise_and)
                    link(nc.vector.tensor_single_scalar(bits[:, 1, :], srcT_i[:, :], 7, ALU.arith_shift_right))
                    link(nc.vector.tensor_copy(lohi[:, :, :], bits[:, :, :]))
                    dve.wait_ge(s_iotax, 1)

                    def factor_hots(g, half):
                        dve.wait_ge(s_hist, g + 1)
                        for k, n, hots in ((1, BLOCKS, hi_hot1), (0, P, lo_hot1)):
                            last = nc.vector.tensor_tensor(hots[:, half, :, :], iota_x[:, 0:n, :],
                                                           lohi[:, k, bass.ds(g * HT, HT)].unsqueeze(1)
                                                           .to_broadcast([P, n, HT]), ALU.is_equal)
                        last.then_inc(s_hot1, 1)

                    with nc.vector.Fori(0, FIRST_TURNS) as j:
                        for q in range(UNROLL):
                            factor_hots(j * UNROLL + q, q % 2)
                    nc.vector.tensor_scalar(idx_tab[:, :], srcT[:, 0:GT], float(N - 1), None, ALU.min)
                    dve.wait_ge(s_basep, 1)
                    link(nc.vector.tensor_tensor(near[0:1, :], base_ps[0:1, 0:GT // TILES], held[0:1, :], ALU.subtract))
                    nc.vector.sem_inc(s_near1, 1)
                    nc.vector.tensor_scalar(base_i[0:1, :], near[0:1, :], 0.0, float(NEAR * P), ALU.max, ALU.min)
                    nc.vector.tensor_tensor(rel[:, :].rearrange("p (g t) -> p g t", t=TILES),
                                            dstT[:, 0:GT].rearrange("p (g t) -> p g t", t=TILES),
                                            base_ps[:, 0:GT // TILES].unsqueeze(2)
                                            .to_broadcast([P, GT // TILES, TILES]), ALU.subtract).then_inc(s_rel, 1)
                    dve.wait_ge(s_wrow, 16 * SETS * WROWS * 2)
                    nc.vector.tensor_single_scalar(wbits[:, 0, :, :], wedge[:, 0, :, :], P - 1, ALU.bitwise_and)
                    nc.vector.tensor_single_scalar(wbits[:, 1, :, :], wedge[:, 0, :, :], 7, ALU.arith_shift_right)
                    for s in range(SETS):
                        last = nc.vector.tensor_scalar(wkey[:, 0, s, :], wedge[:, 1, s, :], thr[:, s:s + 1],
                                                       float(WN), ALU.subtract, ALU.min)
                    link(last)
                    link(nc.vector.tensor_scalar(wkey[:, 0, :, :], wkey[:, 0, :, :], -1.0, float(BLOCKS),
                                                 ALU.max, ALU.mult))
                    nc.vector.tensor_copy(wkey[:, 1, :, :], wbits[:, 0, :, :])
                    nc.vector.tensor_tensor(wkey[:, 0, :, :], wkey[:, 0, :, :], wbits[:, 1, :, :],
                                            ALU.add).then_inc(s_wkey, 1)
                    with nc.vector.Fori(FIRST_TURNS, HIST_GROUPS // UNROLL) as j:
                        for q in range(UNROLL):
                            factor_hots(j * UNROLL + q, q % 2)
                    dve.wait_ge(s_total, 1)
                    link(nc.vector.reduce_sum(total[0:1, :], total_ps[0:1, :], axis=AX_X))
                    nc.vector.tensor_scalar(general[0:1, :], total[0:1, :], float(E + GROUPS), None,
                                            ALU.not_equal).then_inc(s_flag, 1)
                    dve.wait_ge(s_histall, 1)
                    nc.vector.tensor_scalar(deg[:, :], hist_ps[:, 0:BLOCKS], 1.0, None, ALU.max).then_inc(s_deg, 1)
                    dve.wait_ge(s_sqrt, 1)
                    link(nc.vector.reciprocal(rs[:, :], rtmp[:, :]))
                    link(nc.vector.tensor_tensor(rtmp[:, :], rs[:, :], rs[:, :], ALU.mult))
                    link(nc.vector.tensor_tensor(rtmp[:, :], rtmp[:, :], deg[:, :], ALU.mult))
                    link(nc.vector.tensor_scalar(rtmp[:, :], rtmp[:, :], -0.5, 1.5, ALU.mult, ALU.add))
                    dve.wait_ge(s_x, 32)
                    nc.vector.tensor_tensor(rs[:, :], rs[:, :], rtmp[:, :], ALU.mult).then_inc(s_rs, 1)
                    dve.wait_ge(s_rs, 1)
                    for c in range(X_CHUNKS):
                        if c not in HIGH_ON_ACT:
                            for b in range(c * BC, (c + 1) * BC):
                                last = nc.vector.tensor_scalar(yp[:, b, 0, :], xs[:, b, :], rs[:, b:b + 1], None,
                                                               ALU.mult)
                            last.then_inc(s_hi, 1)
                            dve.wait_ge(s_hi, sum(i not in HIGH_ON_ACT for i in range(c + 1)))
                        else:
                            dve.wait_ge(s_hi_act, sum(i in HIGH_ON_ACT for i in range(c + 1)))
                        for b in range(c * BC, (c + 1) * BC):
                            last = nc.vector.scalar_tensor_tensor(out=xs[:, b, :], in0=xs[:, b, :],
                                                                  scalar=rs[:, b:b + 1], in1=yp[:, b, 0, :],
                                                                  op0=ALU.mult, op1=ALU.subtract)
                        last.then_inc(s_r1, 1)
                        if c in LOW_ON_DVE:
                            dve.wait_ge(s_mid, c)
                            b = slice((c - 1) * BC, c * BC)
                            nc.vector.tensor_tensor(yp[:, b, 2, :], xs[:, b, :], yp[:, b, 1, :],
                                                    ALU.subtract).then_inc(s_lo_dve, 1)

                @block.scalar
                def _(act):
                    act.wait_ge(s_edges[0], 48)
                    nc.scalar.copy(edge_f[:, 0, :, :], edge_i[:, 0, :, :]).then_inc(s_edgef_src, 1)
                    for b, (k, c, m) in enumerate(batches):
                        act.wait_ge(s_tr, b + 1)
                        nc.scalar.copy((srcT, dstT)[k][:, c * P:(c + m) * P], tr_ps[:, b % 2, 0:m * P]
                                       ).then_inc(s_trc, 1)
                    act.wait_ge(s_setup, 1)
                    nc.scalar.copy(iota_x[:, :, :], iota_b[:, :].unsqueeze(2).to_broadcast([P, P, HT])
                                   ).then_inc(s_iotax, 1)
                    for s in range(SETS):
                        for k in range(2):
                            b = 2 * s + k
                            act.wait_ge(s_wtr, b + 1)
                            tab = (key_tab, lo_tab)[k][:, s * P * WT:(s + 1) * P * WT]
                            nc.scalar.copy(tab.rearrange("p (w t) -> p t w", t=WT),
                                           wt_ps[:, b % 2, 0:WT * P].rearrange("p (t w) -> p t w", t=WT)
                                           ).then_inc(s_wtc, 1)
                    act.wait_ge(s_deg, 1)
                    nc.scalar.activation(rtmp[:, :], deg[:, :], ACT.Sqrt).then_inc(s_sqrt, 1)
                    act.wait_ge(s_rs, 1)
                    for c in range(X_CHUNKS + 1):
                        if c in HIGH_ON_ACT:
                            for b in range(c * BC, (c + 1) * BC):
                                last = nc.scalar.activation(yp[:, b, 0, :], xs[:, b, :], ACT.Copy,
                                                            scale=rs[:, b:b + 1])
                            last.then_inc(s_hi_act, 1)
                        if c >= 1:
                            act.wait_ge(s_r1, c)
                            nc.scalar.copy(yp[:, (c - 1) * BC:c * BC, 1, :], xs[:, (c - 1) * BC:c * BC, :]
                                           ).then_inc(s_mid, 1)

                @block.tensor
                def _(pe):
                    pe.wait_ge(s_const, 1)
                    for b, (k, c, m) in enumerate(batches):
                        pe.wait_ge(s_edgef if k else s_edgef_src, 1)
                        if b >= 2:
                            pe.wait_ge(s_trc, b - 1)
                        for i in range(m):
                            last = nc.tensor.transpose(tr_ps[:, b % 2, i * P:(i + 1) * P],
                                                       edge_f[:, k, c + i, :], ident[:, :])
                        last.then_inc(s_tr, 1)
                    pe.wait_ge(s_trc, DST_BATCHES)
                    nc.tensor.matmul(base_ps[:, 0:GT // TILES], ones[0:1, :], dstT[0:1, 0:GT:TILES],
                                     start=True, stop=True).then_inc(s_basep, 1)
                    nc.tensor.matmul(below_ps[:, 0:SETS], zeros_b[:, :], zeros_b[:, 0:SETS], start=True, stop=False)
                    for c in range(ROW_CHUNKS):
                        pe.wait_ge(s_below, c + 1)
                        for s in range(SETS):
                            nc.tensor.matmul(below_ps[:, s:s + 1], starts_below[:, c, s * P:(s + 1) * P],
                                             ones_b[:, :], start=False, stop=False, skip_group_check=True)
                    nc.tensor.matmul(below_ps[:, 0:SETS], zeros_b[:, :], zeros_b[:, 0:SETS],
                                     start=False, stop=True).then_inc(s_bcast, 1)
                    nc.tensor.matmul(hist_ps[:, 0:BLOCKS], zeros_b[:, :], zeros_b[:, 0:BLOCKS],
                                     start=True, stop=False)

                    def histogram(g, half):
                        pe.wait_ge(s_hot1, g + 1)
                        for t in range(HT):
                            last = nc.tensor.matmul(hist_ps[:, 0:BLOCKS], lo_hot1[:, half, :, t],
                                                    hi_hot1[:, half, :, t], start=False, stop=False)
                        last.then_inc(s_hist, 1)

                    nc.tensor.sem_inc(s_hist, 2)
                    with nc.tensor.Fori(0, FIRST_TURNS) as j:
                        for q in range(UNROLL):
                            histogram(j * UNROLL + q, q % 2)
                    pe.wait_ge(s_wkey, 1)
                    for s in range(SETS):
                        for k in range(2):
                            b = 2 * s + k
                            if b >= 2:
                                pe.wait_ge(s_wtc, b - 1)
                            for t in range(WT):
                                last = nc.tensor.transpose(wt_ps[:, b % 2, t * P:(t + 1) * P],
                                                           wkey[:, k, s, t * P:(t + 1) * P], ident[:, :])
                            last.then_inc(s_wtr, 1)
                    with nc.tensor.Fori(FIRST_TURNS, HIST_GROUPS // UNROLL) as j:
                        for q in range(UNROLL):
                            histogram(j * UNROLL + q, q % 2)
                    pe.wait_ge(s_masked, 1)
                    for at in range(0, TAKEN, 512):
                        n = min(512, TAKEN - at)
                        last = nc.tensor.matmul(total_ps[0:1, 0:n], ones_b[:, :], taken[:, at:at + n],
                                                start=(at == 0), stop=(at + n == TAKEN))
                    last.then_inc(s_total, 1)
                    nc.tensor.matmul(hist_ps[:, 0:BLOCKS], zeros_b[:, :], zeros_b[:, 0:BLOCKS],
                                     start=False, stop=True).then_inc(s_histall, 1)

        ph2 = ExitStack()
        with ph2:
            def sb2(name, shape, dt):
                return ph2.enter_context(nc.sbuf_tensor(name, shape, dt))

            def ps2(name, shape, dt=F32):
                return ph2.enter_context(nc.psum_tensor(name, shape, dt))

            y_rows = sb2("y_rows", [P, RING, TILES, PARTS * D], BF16)
            idx8 = sb2("idx8", [P, RING, TILES], I32)
            hot = sb2("hot", [P, 2, TILES, W], BF16)
            gT = sb2("gT", [P, 2 * H, NEAR * P + W], F32)
            cnt = sb2("cnt", [1, 2, NEAR * P + W], BF16)
            spread_lo = sb2("spread_lo", [P, WQ * WT, P], F16)
            lo_hot = sb2("lo_hot", [P, 2, WQ * WT, P], F16)
            key_hot = sb2("key_hot", [P, KEY_RING, WT, KEYS], F16)
            counts = sb2("counts", [P, 2, BLOCKS, P], F16)
            zeros = sb2("zeros", [P, H, P], F32)
            gb = sb2("gb", [P, H, P], F32)
            cb = sb2("cb", [1, P], BF16)
            xb = sb2("xb", [P, 2, D], F32)
            has = sb2("has", [P, 2], F32)
            uv = sb2("uv", [P, 2, D], F32)
            uvT = sb2("uvT", [P, 2 * H, P], F32)
            emb = sb2("emb", [P, 2, D], F32)
            ysum = sb2("ysum", [P, 2, D], F32)
            o_sb = sb2("o_sb", [P, D], F32)
            ss = sb2("ss", [P, 2], F32)
            nrm = sb2("nrm", [P, 2], F32)
            inv = sb2("inv", [P, 2], F32)
            stats = sb2("stats", [P, 2, 6], F32)
            mv = sb2("mv", [P, 2, 2], F32)
            veps = sb2("veps", [P, 2], F32)
            std = sb2("std", [P, 2], F32)
            rstd = sb2("rstd", [P, 2], F32)
            grp_ps = ps2("grp_ps", [P, 2, 512])
            win_ps = ps2("win_ps", [P, 2, 512])
            g_ps = ps2("g_ps", [P, 2, 512])
            uvT_ps = ps2("uvT_ps", [P, 512])
            emb_ps = ps2("emb_ps", [P, 512])

            s_zero = sem("s_zero")
            s_idx = sem("s_idx")
            s_rows = [sem(f"s_rows{q}") for q in range(RING)]
            s_hot = sem("s_hot")
            s_grp = sem("s_grp")
            s_acc = sem("s_acc")
            s_spread = sem("s_spread")
            s_lo = sem("s_lo")
            s_key = sem("s_key")
            s_win = sem("s_win")
            s_cnt = sem("s_cnt")
            s_dense = sem("s_dense")
            s_gb = sem("s_gb")
            s_near = sem("s_near")
            s_g0 = sem("s_g0")

            def pair(name):
                return [sem(f"{name}0"), sem(f"{name}1")]

            s_xb = pair("s_xb"); s_uv = pair("s_uv"); s_uvT = pair("s_uvT"); s_uvc = pair("s_uvc")
            s_prod = pair("s_prod"); s_emb = pair("s_emb"); s_sq = pair("s_sq"); s_norm = pair("s_norm")
            s_v = pair("s_v"); s_var = pair("s_var"); s_std = pair("s_std"); s_o = pair("s_o")
            s_out = pair("s_out"); s_stored = pair("s_stored")

            CW = H * W
            STEPS = BG + LAG
            LOOP = (LAG + 1, BD)
            SPLIT = [0] + [BLOCKS * i // (WB - 1) for i in range(WB)]

            def parts_of(j):
                if not isinstance(j, int):
                    return (QUARTERS, True, True, True, True)
                return (max(0, min(QUARTERS, GROUPS - j * QUARTERS)), j < BD, 1 <= j <= BD,
                        LAG <= j < BG + LAG, LAG <= j < BD + LAG)

            def run(engine, step):
                for j in range(LOOP[0]):
                    step(j)
                with engine.Fori(*LOOP) as j:
                    step(j)
                for j in range(LOOP[1], STEPS):
                    step(j)

            def landed(j, q):
                return (j * (QUARTERS // RING) + (q // RING + 1)) * (16 * TILES)

            def turn(j, k):
                n = j - LAG + 1 + (1 - k)
                return min(n, BD + 1) if isinstance(j, int) and k == 0 else n

            def block_of(j, k):
                return j - LAG + k * BG

            with nc.Block() as block:
                @block.sync
                def _(sp):
                    def load(j, k):
                        b = block_of(j, k)
                        n = ROWS_LAST if isinstance(b, int) and b == BLOCKS - 1 else P
                        sp.dma_start(xb[0:n, k, :], x[bass.ds(b * P, n), :]).then_inc(s_xb[k], 16)

                    def step(j):
                        ends = parts_of(j)[3:]
                        for k in (1, 0):
                            if ends[k]:
                                b = block_of(j, k)
                                n = ROWS_LAST if isinstance(b, int) and b == BLOCKS - 1 else P
                                sp.wait_ge(s_o[k], j - LAG + 1)
                                sp.dma_start(out[bass.ds(b * P, n), :], o_sb[0:n, :]).then_inc(s_out[k], 16)
                                if not isinstance(j, int) or parts_of(j + 1)[3 + k]:
                                    load(j + 1, k)
                                sp.wait_ge(s_out[k], (j - LAG) * 16 + 16)
                                sp.sem_inc(s_stored[k], 1)
                    def steps():
                        load(LAG, 1)
                        load(LAG, 0)
                        for k in range(2):
                            sp.sem_inc(s_stored[k], 1)
                        with nc.sync.Fori(LAG, BD) as j:
                            step(j)
                        for j in range(BD, STEPS):
                            step(j)

                    steps()

                @block.gpsimd
                def _(pool):
                    def gathers(j, q):
                        pool.wait_ge(s_idx, j * QUARTERS + (q + 1))
                        nc.gpsimd.nop(nofuse=True)
                        pool.wait_ge(s_grp, j * QUARTERS + (q + 1))
                        nc.gpsimd.nop(nofuse=True)
                        for t in range(TILES):
                            nc.gpsimd.indirect_dma_start(
                                out=y_rows[:, q % RING, t, :], out_offset=None, in_=y_dram[:, :],
                                in_offset=bass.IndirectOffsetOnAxis(ap=idx8[:, q % RING, t:t + 1], axis=0)
                            ).then_inc(s_rows[q % RING], 16)

                    pool.wait_ge(s_ystore, 16 * X_CHUNKS)
                    nc.gpsimd.nop(nofuse=True)
                    with nc.gpsimd.Fori(0, GROUPS // QUARTERS) as j:
                        for q in range(QUARTERS):
                            gathers(j, q)
                    for g in range(GROUPS // QUARTERS * QUARTERS, GROUPS):
                        gathers(g // QUARTERS, g % QUARTERS)

                @block.scalar
                def _(act):
                    def copy_idx(j, q):
                        nc.scalar.copy(idx8[:, q % RING, :], idx_tab[:, bass.ds((j * QUARTERS + q) * TILES, TILES)]
                                       ).then_inc(s_idx, 1)

                    def spread(Q):
                        act.wait_ge(s_lo, Q + 1)
                        nc.scalar.copy(spread_lo[:, :, :],
                                       lo_tab[:, bass.ds(Q * (WQ * WT), WQ * WT)].unsqueeze(2)
                                       .to_broadcast([P, WQ * WT, P])).then_inc(s_spread, 1)

                    def keep_counts(j, i):
                        act.wait_ge(s_win, j * WB + (i + 3))
                        if i == 0:
                            act.wait_ge(s_dense, j + 1)
                        at = counts[:, bass.ds(j % 2, 1), :, i * WN:(i + 1) * WN].rearrange("p o s d -> p (o s) d")
                        nc.scalar.copy(at, win_ps[:, i % 2, 0:KEYS].rearrange("p (d s) -> p s d", s=BLOCKS)
                                       ).then_inc(s_cnt, 1)

                    def block_sums(j):
                        act.wait_ge(s_near, j)
                        act.wait_ge(s_g0, j - LAG + 1)
                        nc.scalar.copy(gb[:, :, :], gT[:, bass.ds((j % 2) * H, H), 0:P]).then_inc(s_gb, 1)
                        nc.scalar.copy(cb[0:1, :], cnt[0:1, bass.ds(j % 2, 1), 0:P].rearrange("p o n -> p (o n)")
                                       ).then_inc(s_gb, 1)

                    def copy_uvT(j, k):
                        act.wait_ge(s_uvT[k], j - LAG + 2)
                        act.wait_ge(s_prod[1 - k], turn(j, k))
                        nc.scalar.copy(uvT[:, :, :], uvT_ps[:, :].rearrange("p (h n) -> p h n", n=P)
                                       ).then_inc(s_uvc[k], 1)

                    def row_norm(j, k):
                        act.wait_ge(s_emb[k], j - LAG + 2)
                        nc.scalar.activation(ysum[:, k, :], emb[:, k, :], ACT.Square, accum_out=ss[:, k:k + 1]
                                             ).then_inc(s_sq[k], 1)
                        act.wait_ge(s_sq[k], j - LAG + 1)
                        nc.scalar.activation(nrm[:, k:k + 1], ss[:, k:k + 1], ACT.Sqrt).then_inc(s_norm[k], 1)

                    def row_std(j, k):
                        act.wait_ge(s_var[k], j - LAG + 1)
                        nc.scalar.activation(std[:, k:k + 1], veps[:, k:k + 1], ACT.Sqrt).then_inc(s_std[k], 1)

                    def step(j):
                        groups, windows, _, end0, end1 = parts_of(j)
                        more = not isinstance(j, int) or (j + 1) < BD
                        for q in range(QUARTERS):
                            for i in range(WQ):
                                if windows:
                                    keep_counts(j, q * WQ + i)
                                if (q, i) == (0, 1) and end0:
                                    block_sums(j)
                                if (q, i) == (0, 3) and end1:
                                    copy_uvT(j, 1)
                                if (q, i) == (1, 2) and end0:
                                    copy_uvT(j, 0)
                                if (q, i) == (2, 0) and end1:
                                    row_norm(j, 1)
                                if i == 1 and windows and (q < QUARTERS - 1 or more):
                                    spread(j * QUARTERS + (q + 2))
                                if (q, i) == (2, 2) and end1:
                                    row_std(j, 1)
                                if (q, i) == (2, 3) and end0:
                                    row_norm(j, 0)
                                if (q, i) == (3, 1) and end0:
                                    row_std(j, 0)
                            if not isinstance(j, int) or j * QUARTERS + q + RING < GROUPS:
                                act.wait_ge(s_rows[q % RING], landed(j, q))
                                copy_idx(j, q + RING)

                    for q in range(RING):
                        copy_idx(0, q)
                    spread(0)
                    spread(1)
                    run(nc.scalar, step)

                @block.tensor
                def _(pe):
                    def group(j, q):
                        g = j * QUARTERS + q
                        pe.wait_ge(s_rows[q % RING], landed(j, q))
                        pe.wait_ge(s_hot, g + 1)
                        pe.wait_ge(s_acc, g + 1)
                        for h in range(H):
                            for t in range(TILES):
                                for m in range(PARTS):
                                    at = m * D + h * P
                                    nc.tensor.matmul(grp_ps[:, q % 2, h * W:(h + 1) * W], y_rows[:, q % RING, t, at:at + P],
                                                     hot[:, q % 2, t, :], start=(t == 0 and m == 0),
                                                     stop=(t == TILES - 1 and m == PARTS - 1))
                        for t in range(TILES):
                            last = nc.tensor.matmul(grp_ps[0:1, q % 2, CW:CW + W], ones_b[:, :], hot[:, q % 2, t, :],
                                                    start=(t == 0), stop=(t == TILES - 1))
                        last.then_inc(s_grp, 1)

                    def window(j, i):
                        if i % WQ == 0:
                            pe.wait_ge(s_lo, j * QUARTERS + (i // WQ + 2))
                        pe.wait_ge(s_key, j * WB + (i + 1))
                        pe.wait_ge(s_cnt, j * WB + (i + 1))
                        for t in range(WT):
                            last = nc.tensor.matmul(win_ps[:, i % 2, 0:KEYS],
                                                    lo_hot[:, (i // WQ) % 2, (i % WQ) * WT + t, :],
                                                    key_hot[:, i % KEY_RING, t, :], start=(t == 0), stop=(t == WT - 1))
                        last.then_inc(s_win, 1)

                    def product(j, i):
                        if i == 1:
                            pe.wait_ge(s_cnt, j * WB + 2)
                            pe.wait_ge(s_uv[1], j)
                        for s in range(SPLIT[i], SPLIT[i + 1]):
                            lhsT = counts[:, bass.ds((j + 1) % 2, 1), s, :].rearrange("p o d -> p (o d)")
                            for m in range(PARTS):
                                nc.tensor.matmul(g_ps[:, 1, 0:D], lhsT, yp[:, s, m, :],
                                                 start=(s == 0 and m == 0), stop=(s == BLOCKS - 1 and m == PARTS - 1))
                            last = nc.tensor.matmul(g_ps[:, 1, D:D + 1], lhsT, ones_b[:, :],
                                                    start=False, stop=(s == BLOCKS - 1), skip_group_check=True)
                        if i == WB - 1:
                            last.then_inc(s_dense, 1)

                    def turn_sums(j):
                        pe.wait_ge(s_gb, 2 * (j - LAG) + 2)
                        pe.wait_ge(s_uv[0], j - LAG + 1)
                        for h in range(H):
                            nc.tensor.transpose(g_ps[:, 0, h * P:(h + 1) * P], gb[:, h, :], ident[:, :])
                        nc.tensor.matmul(g_ps[:, 0, D:D + 1], cb[0:1, :], ones_b[0:1, 0:1],
                                         start=True, stop=True).then_inc(s_g0, 1)

                    def turn_uv(j, k):
                        pe.wait_ge(s_uv[k], j - LAG + 2)
                        pe.wait_ge(s_uvc[1 - k], turn(j, k))
                        for i in range(2):
                            for h in range(H):
                                last = nc.tensor.transpose(uvT_ps[:, (i * H + h) * P:(i * H + h + 1) * P],
                                                           uv[:, i, h * P:(h + 1) * P], ident[:, :])
                        last.then_inc(s_uvT[k], 1)

                    def weights(j, k):
                        pe.wait_ge(s_uvc[k], j - LAG + 2)
                        pe.wait_ge(s_emb[1 - k], turn(j, k))
                        for i, w in enumerate((w1_sb, w2_sb)):
                            for h in range(H):
                                last = nc.tensor.matmul(emb_ps[:, 0:D], uvT[:, i * H + h, :], w[:, h, :],
                                                        start=(i == 0 and h == 0), stop=(i == 1 and h == H - 1))
                        last.then_inc(s_prod[k], 1)

                    def step(j):
                        groups, windows, products, end0, end1 = parts_of(j)
                        for q in range(QUARTERS):
                            late = isinstance(j, int) and j == 0
                            if q < groups and not late:
                                group(j, q)
                            for i in range(q * WQ, (q + 1) * WQ):
                                if windows:
                                    window(j, i)
                                if products:
                                    product(j, i)
                                if i == WQ - 1 and end0:
                                    turn_sums(j)
                                if i == 2 and end1:
                                    turn_uv(j, 1)
                                if i == WQ and end1:
                                    weights(j, 1)
                                if i == WQ + 1 and end0:
                                    turn_uv(j, 0)
                                if i == 2 * WQ - 1 and end0:
                                    weights(j, 0)
                            if q < groups and late:
                                group(j, q)

                    nc.tensor.sem_inc(s_grp, RING)
                    nc.tensor.sem_inc(s_win, 2)
                    nc.tensor.sem_inc(s_dense, 2)
                    nc.tensor.sem_inc(s_g0, 1)
                    for k in range(2):
                        nc.tensor.sem_inc(s_uvT[k], 1)
                        nc.tensor.sem_inc(s_prod[k], 1)
                    run(nc.tensor, step)

                @block.vector
                def _(dve):
                    def one_hots(j, q):
                        g = j * QUARTERS + q
                        dve.wait_ge(s_grp, g + (RING - 1))
                        nc.vector.tensor_tensor(hot[:, q % 2, :, :],
                                                iota_f[:, 0:W].unsqueeze(1).to_broadcast([P, TILES, W]),
                                                rel[:, bass.ds(g * TILES, TILES)].unsqueeze(2).to_broadcast([P, TILES, W]),
                                                ALU.is_equal).then_inc(s_hot, 1)

                    def accumulate(j, g, half):
                        base = nc.vector.value_load(base_i[0:1, bass.ds(g, 1)], min_val=0, max_val=NEAR * P)
                        dve.wait_ge(s_grp, g + (RING + 1))
                        at = gT[:, bass.ds((j % 2) * H, H), bass.ds(base, W)]
                        nc.vector.tensor_tensor(at, at, grp_ps[:, half, 0:CW].rearrange("p (h w) -> p h w", h=H), ALU.add)
                        at = cnt[0:1, bass.ds(j % 2, 1), bass.ds(base, W)].rearrange("p o w -> p (o w)")
                        nc.vector.tensor_tensor(at, at, grp_ps[0:1, half, CW:CW + W], ALU.add).then_inc(s_acc, 1)
                        dve.wait_ge(s_acc, g + 3)

                    def move_on(j):
                        if not isinstance(j, int) or j > LAG:
                            dve.wait_ge(s_gb, 2 * (j - LAG))
                        keep = (NEAR - 1) * P + W
                        new, old = bass.ds((j % 2) * H, H), bass.ds(((j + 1) % 2) * H, H)
                        nc.vector.tensor_copy(gT[:, new, 0:keep], gT[:, old, P:P + keep])
                        nc.vector.tensor_copy(gT[:, new, keep:], zeros[:, :, :])
                        new, old = bass.ds(j % 2, 1), bass.ds((j + 1) % 2, 1)
                        nc.vector.tensor_copy(cnt[0:1, new, 0:keep], cnt[0:1, old, P:P + keep])
                        nc.vector.tensor_copy(cnt[0:1, new, keep:], zeros[0:1, 0:1, :]).then_inc(s_near, 1)
                        dve.wait_ge(s_near, j)

                    def place_hots(Q, half):
                        dve.wait_ge(s_spread, Q + 1)
                        if not isinstance(Q, int) or Q > 1:
                            dve.wait_ge(s_win, Q * WQ - (WQ - 2))
                        nc.vector.tensor_tensor(lo_hot[:, half, :, :],
                                                iota_h[:, 0:P].unsqueeze(1).to_broadcast([P, WQ * WT, P]),
                                                spread_lo[:, :, :], ALU.is_equal).then_inc(s_lo, 1)

                    def key_hots(j, i):
                        if not isinstance(j, int) or j * WB + i >= KEY_RING:
                            dve.wait_ge(s_win, j * WB + (i + 3 - KEY_RING))
                        for t in range(WT):
                            last = nc.vector.tensor_scalar(key_hot[:, i % KEY_RING, t, :], iota_h[:, :],
                                                           key_tab[:, bass.ds((j * WB + i) * WT + t, 1)], None,
                                                           ALU.is_equal)
                        last.then_inc(s_key, 1)

                    def sums(j, k):
                        b = block_of(j, k)
                        if k == 0:
                            dve.wait_ge(s_g0, j - LAG + 2)
                        else:
                            dve.wait_ge(s_dense, j + 1)
                        dve.wait_ge(s_xb[k], (j - LAG) * 16 + 16)
                        dve.wait_ge(s_uvT[1 - k], turn(j, k))
                        nc.vector.tensor_scalar(has[:, k:k + 1], g_ps[:, k, D:D + 1], 0.0, None, ALU.is_gt)
                        nc.vector.scalar_tensor_tensor(out=uv[:, 0, :], in0=g_ps[:, k, 0:D],
                                                       scalar=rs[:, bass.ds(b, 1)], in1=xb[:, k, :],
                                                       op0=ALU.mult, op1=ALU.add)
                        nc.vector.scalar_tensor_tensor(out=uv[:, 1, :], in0=g_ps[:, k, 0:D],
                                                       scalar=rs[:, bass.ds(b, 1)], in1=xb[:, k, :],
                                                       op0=ALU.mult, op1=ALU.mult).then_inc(s_uv[k], 1)

                    LINKS = 8

                    def link(ins, j, k, at):
                        ins.then_inc(s_v[k], 1)
                        dve.wait_ge(s_v[k], (j - LAG) * LINKS + at)

                    def embed(j, k):
                        dve.wait_ge(s_prod[k], j - LAG + 2)
                        link(nc.vector.scalar_tensor_tensor(out=emb[:, k, :], in0=emb_ps[:, 0:D], scalar=has[:, k:k + 1],
                                                            in1=bias_sb[:, :], op0=ALU.mult, op1=ALU.add), j, k, 1)
                        nc.vector.scalar_tensor_tensor(out=emb[:, k, :], in0=emb[:, k, :], scalar=0.01,
                                                       in1=emb[:, k, :], op0=ALU.mult, op1=ALU.max).then_inc(s_emb[k], 1)

                    def residual(j, k):
                        dve.wait_ge(s_norm[k], j - LAG + 1)
                        link(nc.vector.tensor_scalar(nrm[:, k:k + 1], nrm[:, k:k + 1], 1e-12, None, ALU.max), j, k, 2)
                        link(nc.vector.reciprocal(inv[:, k:k + 1], nrm[:, k:k + 1]), j, k, 3)
                        link(nc.vector.scalar_tensor_tensor(out=ysum[:, k, :], in0=emb[:, k, :], scalar=inv[:, k:k + 1],
                                                            in1=xb[:, k, :], op0=ALU.mult, op1=ALU.add), j, k, 4)
                        link(nc.vector.bn_stats(stats[:, k, :], ysum[:, k, :]), j, k, 5)
                        nc.vector.nop(nofuse=True)
                        link(nc.vector.bn_aggr(mv[:, k, :], stats[:, k, :]), j, k, 6)
                        nc.vector.tensor_scalar(veps[:, k:k + 1], mv[:, k, 1:2], 1e-5, None, ALU.add).then_inc(s_var[k], 1)

                    def layer_norm(j, k):
                        dve.wait_ge(s_std[k], j - LAG + 1)
                        link(nc.vector.reciprocal(rstd[:, k:k + 1], std[:, k:k + 1]), j, k, 7)
                        dve.wait_ge(s_stored[1 - k], turn(j, k))
                        nc.vector.tensor_scalar(o_sb[:, :], ysum[:, k, :], mv[:, k, 0:1], rstd[:, k:k + 1],
                                                ALU.subtract, ALU.mult).then_inc(s_o[k], 1)
                        nc.vector.sem_inc(s_v[k], 1)

                    def step(j):
                        groups, windows, _, end0, end1 = parts_of(j)
                        for q in range(QUARTERS):
                            i = q * WQ
                            if windows:
                                key_hots(j, i)
                            if q < groups:
                                one_hots(j, q + 1)
                            if q == 1 and end0:
                                sums(j, 0)
                            if q == 3 and end1:
                                layer_norm(j, 1)
                            if windows:
                                key_hots(j, i + 1)
                            if q == 0 and end1:
                                sums(j, 1)
                            if q == 3 and end0:
                                residual(j, 0)
                            if not isinstance(j, int) or 0 < j * QUARTERS + q <= GROUPS:
                                accumulate(j - 1 if q == 0 else j, j * QUARTERS + q - 1, (q + 1) % 2)
                            if q == 0 and (not isinstance(j, int) or j > 0):
                                move_on(j)
                            if windows:
                                key_hots(j, i + 2)
                            if windows and (q < QUARTERS - 1 or not isinstance(j, int) or j + 1 < BD):
                                place_hots(j * QUARTERS + (q + 1), (q + 1) % 2)
                            if q == 2 and end1:
                                residual(j, 1)
                            if q == 2 and end0:
                                embed(j, 0)
                            if windows:
                                key_hots(j, i + 3)
                            if q == 1 and end1:
                                embed(j, 1)
                            if q == 3 and end0:
                                layer_norm(j, 0)

                    nc.vector.memset(gT[:, :, :], 0.0)
                    nc.vector.memset(zeros[:, :, :], 0.0)
                    nc.vector.memset(cnt[:, :, :], 0.0)
                    nc.vector.engine_nop().then_inc(s_zero, 1)
                    dve.wait_ge(s_zero, 1)
                    nc.vector.sem_inc(s_acc, 2)
                    nc.vector.sem_inc(s_lo, 1)
                    nc.vector.sem_inc(s_cnt, 2)
                    for k in range(2):
                        nc.vector.sem_inc(s_uv[k], 1)
                        nc.vector.sem_inc(s_uvc[k], 1)
                        nc.vector.sem_inc(s_emb[k], 1)
                    one_hots(0, 0)
                    place_hots(0, 0)
                    run(nc.vector, step)


        ph3 = ExitStack()
        with ph3:
            def sb3(name, shape, dt):
                return ph3.enter_context(nc.sbuf_tensor(name, shape, dt))

            def ps3(name, shape):
                return ph3.enter_context(nc.psum_tensor(name, shape, F32))

            PASSES = BLOCKS // SPAN
            NODES = SPAN * P
            LISTS = next(n for n in range(P, 0, -1) if E % n == 0 and E // n % (SLOTS * BATCH) == 0)
            EDGES = E // LISTS
            TURNS = EDGES // (SLOTS * BATCH)
            BATCHES = TURNS * SLOTS
            LINKS3 = 8
            assert PASSES * SPAN == BLOCKS

            p_src = sb3("p_src", [P, EDGES], I32)
            p_dsti = sb3("p_dsti", [P, EDGES], I32)
            p_dst = sb3("p_dst", [P, EDGES], F32)
            p_iotai = sb3("p_iotai", [P, NODES], I32)
            p_iota = sb3("p_iota", [P, NODES], F16)
            p_zeros = sb3("p_zeros", [P, D + 1], BF16)
            p_rownum = sb3("p_rownum", [P, SLOTS, BATCH], I32)
            p_rows = sb3("p_rows", [P, SLOTS, BATCH, PARTS * D], BF16)
            p_hot = sb3("p_hot", [P, 2, BATCH, NODES], F16)
            p_x = sb3("p_x", [P, D], F32)
            p_has = sb3("p_has", [P, 1], F32)
            p_uv = sb3("p_uv", [P, 2, D], F32)
            p_uvT = sb3("p_uvT", [P, 2 * H, P], F32)
            p_emb = sb3("p_emb", [P, D], F32)
            p_y = sb3("p_y", [P, D], F32)
            p_out = sb3("p_out", [P, D], F32)
            p_ss = sb3("p_ss", [P, 1], F32)
            p_norm = sb3("p_norm", [P, 1], F32)
            p_inv = sb3("p_inv", [P, 1], F32)
            p_stats = sb3("p_stats", [P, 6], F32)
            p_mv = sb3("p_mv", [P, 2], F32)
            p_veps = sb3("p_veps", [P, 1], F32)
            p_std = sb3("p_std", [P, 1], F32)
            p_rstd = sb3("p_rstd", [P, 1], F32)
            sum_ps = ps3("sum_ps", [P, SPAN, 512])
            turn_ps = ps3("turn_ps", [P, 512])

            q_pad = sem("q_pad"); q_edges = sem("q_edges"); q_iota = sem("q_iota"); q_setup = sem("q_setup")
            q_zeros = sem("q_zeros")
            q_num = sem("q_num")
            q_rows = [sem(f"q_rows{b}") for b in range(SLOTS)]
            q_hot = sem("q_hot")
            q_batch = sem("q_batch")
            q_move = sem("q_move")
            q_sums = sem("q_sums")
            q_x = sem("q_x"); q_uv = sem("q_uv"); q_turned = sem("q_turned"); q_uvT = sem("q_uvT")
            q_prod = sem("q_prod"); q_emb = sem("q_emb"); q_sq = sem("q_sq"); q_norm = sem("q_norm")
            q_v = sem("q_v"); q_var = sem("q_var"); q_std = sem("q_std"); q_out = sem("q_out")
            q_done = sem("q_done"); q_stored = sem("q_stored")

            def run_passes(engine, one_pass):
                with engine.Fori(0, PASSES - 1) as p:
                    one_pass(p)
                one_pass(PASSES - 1)

            def run_batches(engine, p, batch):
                with engine.Fori(0, TURNS) as t:
                    for b in range(SLOTS):
                        batch(p * TURNS + t, (p * TURNS + t) * SLOTS + b, b, t)

            def rows_of(p, i):
                return ROWS_LAST if isinstance(p, int) and p * SPAN + i == BLOCKS - 1 else P

            def when_general(engine):
                flag = engine.value_load(general[0:1, 0:1], min_val=0, max_val=1)
                return engine.If(flag > 0)

            with nc.Block() as block:
                @block.sync
                def _(sp):
                    with when_general(nc.sync):
                        sp.wait_ge(q_pad, 1)
                        sp.dma_start(p_src[0:LISTS, :], src.rearrange("(q e) -> q e", e=EDGES)).then_inc(q_edges, 16)
                        sp.dma_start(p_dsti[0:LISTS, :], dst.rearrange("(q e) -> q e", e=EDGES)).then_inc(q_edges, 16)
                        sp.wait_ge(q_edges, 32)

                        def stores(p):
                            for i in range(SPAN):
                                at = p * (SPAN * P) + i * P
                                n = rows_of(p, i)
                                sp.dma_start(p_x[0:n, :], x[bass.ds(at, n), :]).then_inc(q_x, 16)
                                sp.wait_ge(q_out, p * SPAN + (i + 1))
                                sp.dma_start(out[bass.ds(at, n), :], p_out[0:n, :]).then_inc(q_done, 16)
                                sp.wait_ge(q_done, (p * SPAN + (i + 1)) * 16)
                                sp.sem_inc(q_stored, 1)

                        sp.sem_inc(q_stored, 1)
                        run_passes(nc.sync, stores)

                @block.gpsimd
                def _(pool):
                    with when_general(nc.gpsimd):
                        nc.gpsimd.memset(p_src[:, :], 0)
                        nc.gpsimd.memset(p_dsti[:, :], PAD_ID)
                        nc.gpsimd.memset(p_x[:, :], 0.0)
                        nc.gpsimd.drain().then_inc(q_pad, 1)
                        nc.gpsimd.iota(p_iotai[:, :], pattern=[[1, NODES]], base=0,
                                       channel_multiplier=0).then_inc(q_iota, 1)

                        def gathers(turn, n, slot, t):
                            pool.wait_ge(q_num, n + 1)
                            nc.gpsimd.nop(nofuse=True)
                            pool.wait_ge(q_batch, n + 1)
                            nc.gpsimd.nop(nofuse=True)
                            for k in range(BATCH):
                                nc.gpsimd.indirect_dma_start(
                                    out=p_rows[:, slot, k, :], out_offset=None, in_=y_dram[:, :],
                                    in_offset=bass.IndirectOffsetOnAxis(ap=p_rownum[:, slot, k:k + 1], axis=0)
                                ).then_inc(q_rows[slot], 16)

                        run_passes(nc.gpsimd, lambda p: run_batches(nc.gpsimd, p, gathers))

                @block.scalar
                def _(act):
                    with when_general(nc.scalar):
                        act.wait_ge(q_edges, 32)

                        def numbers(turn, n, slot, t):
                            act.wait_ge(q_batch, n + 1)
                            nc.scalar.copy(p_rownum[:, slot, :],
                                           p_src[:, bass.ds(t * (SLOTS * BATCH) + slot * BATCH, BATCH)]
                                           ).then_inc(q_num, 1)

                        def ends(p):
                            run_batches(nc.scalar, p, numbers)
                            for i in range(SPAN):
                                n = p * SPAN + i
                                act.wait_ge(q_turned, n + 1)
                                nc.scalar.copy(p_uvT[:, :, :], turn_ps[:, :].rearrange("p (h n) -> p h n", n=P)
                                               ).then_inc(q_uvT, 1)
                                act.wait_ge(q_emb, n + 2)
                                nc.scalar.activation(p_y[:, :], p_emb[:, :], ACT.Square, accum_out=p_ss[:, :]
                                                     ).then_inc(q_sq, 1)
                                act.wait_ge(q_sq, n + 1)
                                nc.scalar.activation(p_norm[:, :], p_ss[:, :], ACT.Sqrt).then_inc(q_norm, 1)
                                act.wait_ge(q_var, n + 1)
                                nc.scalar.activation(p_std[:, :], p_veps[:, :], ACT.Sqrt).then_inc(q_std, 1)

                        run_passes(nc.scalar, ends)

                @block.tensor
                def _(pe):
                    with when_general(nc.tensor):
                        def batch(turn, n, slot, t):
                            pe.wait_ge(q_rows[slot], turn * (16 * BATCH) + 16 * BATCH)
                            pe.wait_ge(q_hot, n + 1)
                            for k in range(BATCH):
                                for i in range(SPAN):
                                    lhsT = p_hot[:, slot % 2, k, i * P:(i + 1) * P]
                                    for m in range(PARTS):
                                        nc.tensor.matmul(sum_ps[:, i, 0:D], lhsT, p_rows[:, slot, k, m * D:(m + 1) * D],
                                                         start=False, stop=False, skip_group_check=True)
                                    last = nc.tensor.matmul(sum_ps[:, i, D:D + 1], lhsT, ones_b[:, :],
                                                            start=False, stop=False, skip_group_check=True)
                            last.then_inc(q_batch, 1)

                        def blocks(p):
                            pe.wait_ge(q_emb, p * SPAN + 1)
                            for i in range(SPAN):
                                nc.tensor.matmul(sum_ps[:, i, 0:D + 1], p_zeros[:, 0:P], p_zeros[:, :],
                                                 start=True, stop=False, skip_group_check=True)
                            run_batches(nc.tensor, p, batch)
                            for i in range(SPAN):
                                last = nc.tensor.matmul(sum_ps[:, i, 0:D + 1], p_zeros[:, 0:P], p_zeros[:, :],
                                                        start=False, stop=True, skip_group_check=True)
                            last.then_inc(q_sums, 1)
                            for i in range(SPAN):
                                n = p * SPAN + i
                                pe.wait_ge(q_uv, n + 1)
                                for a in range(2):
                                    for h in range(H):
                                        last = nc.tensor.transpose(turn_ps[:, (a * H + h) * P:(a * H + h + 1) * P],
                                                                   p_uv[:, a, h * P:(h + 1) * P], ident[:, :])
                                last.then_inc(q_turned, 1)
                                pe.wait_ge(q_uvT, n + 1)
                                for a, w in enumerate((w1_sb, w2_sb)):
                                    for h in range(H):
                                        last = nc.tensor.matmul(sum_ps[:, i, 0:D], p_uvT[:, a * H + h, :], w[:, h, :],
                                                                start=(a == 0 and h == 0), stop=(a == 1 and h == H - 1))
                                last.then_inc(q_prod, 1)

                        nc.tensor.sem_inc(q_batch, SLOTS)
                        pe.wait_ge(q_zeros, 1)
                        run_passes(nc.tensor, blocks)

                @block.vector
                def _(dve):
                    with when_general(nc.vector):
                        def one_hots(turn, n, slot, t):
                            dve.wait_ge(q_batch, n + (SLOTS - 1))
                            for k in range(BATCH):
                                last = nc.vector.tensor_scalar(
                                    p_hot[:, slot % 2, k, :], p_iota[:, :],
                                    p_dst[:, bass.ds(t * (SLOTS * BATCH) + (slot * BATCH + k), 1)], None, ALU.is_equal)
                            last.then_inc(q_hot, 1)

                        def link(ins, n, at):
                            ins.then_inc(q_v, 1)
                            dve.wait_ge(q_v, n * LINKS3 + at)

                        def ends(p):
                            run_batches(nc.vector, p, one_hots)
                            dve.wait_ge(q_sums, p + 1)
                            for i in range(SPAN):
                                n = p * SPAN + i
                                dve.wait_ge(q_x, n * 16 + 16)
                                nc.vector.tensor_scalar(p_has[:, :], sum_ps[:, i, D:D + 1], 0.0, None, ALU.is_gt)
                                for a, op in enumerate((ALU.add, ALU.mult)):
                                    last = nc.vector.scalar_tensor_tensor(
                                        out=p_uv[:, a, :], in0=sum_ps[:, i, 0:D], scalar=rs[:, bass.ds(n, 1)],
                                        in1=p_x[:, :], op0=ALU.mult, op1=op)
                                last.then_inc(q_uv, 1)
                                dve.wait_ge(q_prod, n + 1)
                                link(nc.vector.scalar_tensor_tensor(
                                    out=p_emb[:, :], in0=sum_ps[:, i, 0:D], scalar=p_has[:, :], in1=bias_sb[:, :],
                                    op0=ALU.mult, op1=ALU.add), n, 1)
                                nc.vector.scalar_tensor_tensor(
                                    out=p_emb[:, :], in0=p_emb[:, :], scalar=0.01, in1=p_emb[:, :],
                                    op0=ALU.mult, op1=ALU.max).then_inc(q_emb, 1)
                                dve.wait_ge(q_norm, n + 1)
                                link(nc.vector.tensor_scalar(p_norm[:, :], p_norm[:, :], 1e-12, None, ALU.max), n, 2)
                                link(nc.vector.reciprocal(p_inv[:, :], p_norm[:, :]), n, 3)
                                link(nc.vector.scalar_tensor_tensor(
                                    out=p_y[:, :], in0=p_emb[:, :], scalar=p_inv[:, :], in1=p_x[:, :],
                                    op0=ALU.mult, op1=ALU.add), n, 4)
                                link(nc.vector.bn_stats(p_stats[:, :], p_y[:, :]), n, 5)
                                nc.vector.nop(nofuse=True)
                                link(nc.vector.bn_aggr(p_mv[:, :], p_stats[:, :]), n, 6)
                                nc.vector.tensor_scalar(p_veps[:, :], p_mv[:, 1:2], 1e-5, None,
                                                        ALU.add).then_inc(q_var, 1)
                                dve.wait_ge(q_std, n + 1)
                                link(nc.vector.reciprocal(p_rstd[:, :], p_std[:, :]), n, 7)
                                dve.wait_ge(q_stored, n + 1)
                                nc.vector.tensor_scalar(p_out[:, :], p_y[:, :], p_mv[:, 0:1], p_rstd[:, :],
                                                        ALU.subtract, ALU.mult).then_inc(q_out, 1)
                                nc.vector.sem_inc(q_v, 1)
                            nc.vector.tensor_scalar(p_dst[:, :], p_dst[:, :], float(NODES), None,
                                                    ALU.subtract).then_inc(q_move, 1)
                            dve.wait_ge(q_move, p + 1)

                        nc.vector.memset(p_zeros[:, :], 0.0).then_inc(q_zeros, 1)
                        nc.vector.sem_inc(q_emb, 1)
                        dve.wait_ge(q_iota, 1)
                        nc.vector.tensor_copy(p_iota[:, :], p_iotai[:, :])
                        dve.wait_ge(q_edges, 32)
                        nc.vector.tensor_copy(p_dst[:, :], p_dsti[:, :]).then_inc(q_setup, 1)
                        dve.wait_ge(q_setup, 1)
                        run_passes(nc.vector, ends)


_INS = ['x', 'src', 'dst', 'L0_gnn_W1', 'L0_gnn_W2', 'L0_gnn_b']


def kernel(**inputs):
    import numpy as _np
    import concourse.bacc as _bacc
    from concourse import mybir as _mybir
    from concourse.bass_utils import run_bass_kernel_spmd as _run

    nc = _bacc.Bacc("TRN2", target_bir_lowering=False, num_devices=1)
    arrays, args = {}, []
    for name in _INS:
        a = _np.ascontiguousarray(inputs[name])
        arrays[f"in_{name}_dram"] = a
        args.append(nc.dram_tensor(f"in_{name}_dram", a.shape, _mybir.dt.from_np(a.dtype), kind="ExternalInput").ap())
    shape = tuple(inputs['x'].shape)
    args.append(nc.dram_tensor("out_0_dram", shape, _mybir.dt.float32, kind="ExternalOutput").ap())
    build(nc, *args)
    r = _run(nc, [arrays], core_ids=[0])
    return r.results[0]["out_0_dram"]
```

```python
from contextlib import ExitStack

import concourse.bass as bass
from concourse import mybir

F32 = mybir.dt.float32
BF16 = mybir.dt.bfloat16
I32 = mybir.dt.int32
U16 = mybir.dt.uint16
F16 = mybir.dt.float16
ALU = mybir.AluOpType
ACT = mybir.ActivationFunctionType
AX_X = mybir.AxisListType.X

P = 128
TILES = 8
RING = 4
QUARTERS = 4
W = 48
NEAR = 4
LAG = 2
LEAD = 2
GATHER_BLOCKS = 23
LIST_N = 4
LIST_T = 2
LISTS_W = 2
KEY_RING = 4
EROW = 64
PAD_ID = 8191
PARTS = 3
X_CHUNKS = 7
HT = 16
UNROLL = 20
FIRST_TURNS = 2
HI_RING = 4
STEP_LEAD = 8
SIGN_GROUPS = (4, 9, 14, 19)
HIGH_ON_ACT = (1, 3, 4, 6)
LOW_ON_DVE = (6,)
SPAN = 7
BATCH = 4
SLOTS = 8


def build(nc, x, src, dst, w1, w2, bias, out):
    N, D = x.shape
    E = src.shape[0]
    H = D // P
    BLOCKS = -(-N // P)
    BG = GATHER_BLOCKS
    BD = BLOCKS - BG
    ROWS_LAST = N - (BLOCKS - 1) * P
    HIST_GROUPS = -(-E // (P * HT * UNROLL)) * UNROLL
    GROUPS = BG * QUARTERS + 1
    TC = -(-HIST_GROUPS * HT // P)
    TT = TC * P
    GT = -(-(GROUPS + 1) // QUARTERS) * QUARTERS * TILES
    FULL_CHUNKS = E // (P * P)
    REST_ROWS, REST_EDGES = divmod(E - FULL_CHUNKS * P * P, P)
    BC = BLOCKS // X_CHUNKS
    WN = LISTS_W * LIST_N
    WT = LISTS_W * LIST_T
    WB = P // WN
    WQ = WB // QUARTERS
    SETS = -(-BD * WB * LISTS_W // P)
    WE = LIST_T * P
    WROWS = WE // EROW
    ND0 = BG * P
    LKEYS = LIST_N * BLOCKS
    KEYS = LISTS_W * LKEYS
    TAB = SETS * P * LIST_T
    assert TAB >= (BD * WB + 2 * WQ) * WT and SETS * LIST_N < P and E % EROW == 0
    ROW_CHUNKS = TC * P // EROW
    SET_N = P * LIST_N
    assert SET_N & (SET_N - 1) == 0
    TAKEN = GROUPS * TILES + SETS * WE + GROUPS

    y_dram = nc.dram_tensor("y_parts", [BLOCKS * P, PARTS * D], BF16, kind="Internal").ap()

    ctx = ExitStack()
    with ctx:
        def sb(name, shape, dt):
            return ctx.enter_context(nc.sbuf_tensor(name, shape, dt))

        def sem(name):
            return ctx.enter_context(nc.semaphore(name))

        ident = sb("ident", [P, P], F32)
        ones = sb("ones", [P, P], F32)
        ones_b = sb("ones_b", [P, 1], BF16)
        iota_f = sb("iota_f", [P, W], F32)
        iota_h = sb("iota_h", [P, LKEYS], F16)
        w1_sb = sb("w1_sb", [P, H, D], F32)
        w2_sb = sb("w2_sb", [P, H, D], F32)
        bias_sb = sb("bias_sb", [P, D], F32)
        idx_tab = sb("idx_tab", [P, GT], U16)
        rel = sb("rel", [P, GT], F16)
        base_i = sb("base_i", [1, GT // TILES], I32)
        key_tab = sb("key_tab", [P, TAB], F16)
        lo_tab = sb("lo_tab", [P, TAB], F16)
        rs = sb("rs", [P, BLOCKS], F32)
        yp_1 = sb("yp_1", [P, BLOCKS, PARTS * D + 2], BF16)
        yp = yp_1[:, :, 0:PARTS * D].rearrange("p b (k d) -> p b k d", k=PARTS)
        general = sb("general", [1, 1], I32)

        s_pad = sem("s_pad"); s_const = sem("s_const"); s_w = sem("s_w"); s_edges = [sem("s_edges_src"), sem("s_edges_dst")]
        s_x = sem("s_x"); s_edgef = sem("s_edgef"); s_tr = sem("s_tr"); s_trc = sem("s_trc")
        s_basep = sem("s_basep"); s_setup = sem("s_setup"); s_bcast = sem("s_bcast")
        s_widx = sem("s_widx"); s_wrow = sem("s_wrow"); s_wkey = sem("s_wkey")
        s_wtr = sem("s_wtr"); s_wtc = sem("s_wtc"); s_hot1 = sem("s_hot1")
        s_hist = sem("s_hist"); s_histall = sem("s_histall"); s_deg = sem("s_deg"); s_sqrt = sem("s_sqrt")
        s_hi = sem("s_hi"); s_r1 = sem("s_r1"); s_mid = sem("s_mid"); s_lo3 = sem("s_lo3")
        s_hi_act = sem("s_hi_act"); s_lo_dve = sem("s_lo_dve"); s_rs = sem("s_rs"); s_iotax = sem("s_iotax")
        s_differ = sem("s_differ"); s_bits = sem("s_bits"); s_half = sem("s_half"); s_step = sem("s_step")
        s_steps = sem("s_steps"); s_stepsum = sem("s_stepsum")
        s_edgef_src = sem("s_edgef_src"); s_below = sem("s_below")
        s_ystore = sem("s_ystore"); s_wpad = sem("s_wpad")
        s_near1 = sem("s_near1"); s_rel = sem("s_rel"); s_mask = sem("s_mask"); s_masked = sem("s_masked")
        s_total = sem("s_total"); s_flag = sem("s_flag")

        ph1 = ExitStack()
        with ph1:
            def sb1(name, shape, dt):
                return ph1.enter_context(nc.sbuf_tensor(name, shape, dt))

            iota_i = sb1("iota_i", [P, LKEYS], I32)
            edge_i = sb1("edge_i", [P, 2, TC, P], I32)
            edge_f = sb1("edge_f", [P, 2, TC, P], F32)
            srcT = sb1("srcT", [P, TT], F32)
            dstT = sb1("dstT", [P, TT], F32)
            srcT_i = edge_i[:, 0, :, :].rearrange("p c e -> p (c e)")
            bits = edge_f[:, :, :, :].bitcast(I32).rearrange("p k c e -> p k (c e)")
            lohi = sb1("lohi", [P, 2, TT], BF16)
            iota_b = sb1("iota_b", [P, P], BF16)
            iota_x = sb1("iota_x", [P, P, HT], BF16)
            lo_hot1 = sb1("lo_hot1", [P, 2, P, HT], BF16)
            step_sums = sb1("step_sums", [P, BLOCKS], F32)
            hi_hot1 = sb1("hi_hot1", [P, HI_RING, BLOCKS, HT], BF16)
            zeros_b = sb1("zeros_b", [P, P], BF16)
            xs = sb1("xs", [P, BLOCKS, D], F32)
            deg = sb1("deg", [P, BLOCKS], F32)
            rtmp = sb1("rtmp", [P, BLOCKS], F32)
            thr_i = sb1("thr_i", [P, SETS], I32)
            thr = sb1("thr", [P, SETS], F32)
            held_i = sb1("held_i", [1, GT // TILES], I32)
            held = sb1("held", [1, GT // TILES], F32)
            near = sb1("near", [1, GT // TILES], F32)
            start_h = sb1("start_h", [P, P], F16)
            ones_w = sb1("ones_w", [P, P], BF16)
            first = sb1("first", [P, SETS], F32)
            widx = sb1("widx", [P, SETS, WROWS], I32)
            total = sb1("total", [1, 1], F32)
            words = yp_1[:, :, :].rearrange("p b e -> p (b e)").bitcast(I32)
            WWORDS = 2 * SETS * WE
            wedge, wbits, wkey = (words[:, i * WWORDS:(i + 1) * WWORDS].rearrange("p (k s e) -> p k s e", k=2, s=SETS)
                                  for i in range(3))
            wkey = wkey.bitcast(F32)
            free = words[:, 3 * WWORDS:].bitcast(F32)
            in_group = free[:, 0:GROUPS * TILES]
            in_window = free[:, GROUPS * TILES:GROUPS * TILES + SETS * WE]
            half_lo = words[:, -TT:].bitcast(F32)
            lo_step = words[:, -TT - HT * P:-TT].bitcast(BF16).rearrange("p (k t n) -> p k t n", k=2, t=HT)
            taken = free[:, GROUPS * TILES + SETS * WE:].bitcast(BF16)[:, 0:TAKEN]
            in_reach = words[0:1, -TT - HT * P - 3 * P:].bitcast(F32)[:, 0:GROUPS]
            assert GROUPS <= P and 3 * WWORDS + GROUPS * TILES + SETS * WE + TAKEN // 2 + 1 <= (
                BLOCKS * (PARTS * D + 2) // 2 - TT - HT * P - 3 * P)
            differ = words[:, -TT - HT * P - P:-TT - HT * P].bitcast(F32)
            starts_below = free[:, 0:ROW_CHUNKS * P // 2].bitcast(BF16).rearrange("p (c w) -> p c w", w=P)
            found = words[:, 3 * WWORDS + ROW_CHUNKS * P // 2:]
            start_i = found[:, -TT - HT * P - 2 * P:-TT - HT * P - P]
            row_i = found[:, 0:ROW_CHUNKS]
            row_bits = found[:, ROW_CHUNKS:3 * ROW_CHUNKS].rearrange("p (k c) -> p k c", k=2)
            row_h = found[:, 3 * ROW_CHUNKS:4 * ROW_CHUNKS].bitcast(F16).rearrange("p (k c) -> p k c", k=2)
            in_set, before_set = (found[:, at:at + ROW_CHUNKS * SETS // 2].bitcast(BF16)
                                  .rearrange("p (c s) -> p c s", s=SETS)
                                  for at in (4 * ROW_CHUNKS, 4 * ROW_CHUNKS + ROW_CHUNKS * SETS // 2))


            def ps1(name, shape):
                return ph1.enter_context(nc.psum_tensor(name, shape, F32))

            tr_ps = ps1("tr_ps", [P, 2, 512])
            base_ps = ps1("base_ps", [P, 512])
            hist_ps = ps1("hist_ps", [P, 512])
            below_ps = ps1("below_ps", [P, 512])
            step_ps = ps1("step_ps", [P, 512])
            wt_ps = ps1("wt_ps", [P, 2, 512])
            total_ps = base_ps

            batches = [(s, c, min(4, TC - c)) for s in (1, 0) for c in range(0, TC, 4)]
            DST_BATCHES = len(batches) // 2
            assert UNROLL % HI_RING == 0 and (UNROLL - len(SIGN_GROUPS)) % 2 == 0 and len(SIGN_GROUPS) % 2 == 0
            after_two = SIGN_GROUPS[2:] + tuple(q + UNROLL for q in SIGN_GROUPS)
            assert SIGN_GROUPS[0] >= STEP_LEAD - HI_RING
            assert all(b >= a + STEP_LEAD for a, b in zip(SIGN_GROUPS, after_two))

            with nc.Block() as block:
                @block.sync
                def _(sp):
                    sp.wait_ge(s_pad, 1)
                    for k, e in ((1, dst), (0, src)):
                        sp.dma_start(edge_i[:, k, 0:FULL_CHUNKS, :],
                                     e[0:FULL_CHUNKS * P * P].rearrange("(c q e) -> q c e", q=P, e=P)
                                     ).then_inc(s_edges[k], 16)
                        at = FULL_CHUNKS * P * P
                        sp.dma_start(edge_i[0:REST_ROWS, k, FULL_CHUNKS, :],
                                     e[at:at + REST_ROWS * P].rearrange("(q e) -> q e", e=P)
                                     ).then_inc(s_edges[k], 16)
                        at += REST_ROWS * P
                        sp.dma_start(edge_i[REST_ROWS:REST_ROWS + 1, k, FULL_CHUNKS, 0:REST_EDGES],
                                     e[at:at + REST_EDGES].rearrange("(o e) -> o e", o=1)
                                     ).then_inc(s_edges[k], 16)
                    sp.dma_start(xs[:, 0:BLOCKS - 1, :],
                                 x[0:(BLOCKS - 1) * P, :].rearrange("(c p) d -> p c d", p=P)).then_inc(s_x, 16)
                    sp.dma_start(xs[0:ROWS_LAST, BLOCKS - 1, :], x[(BLOCKS - 1) * P:N, :]).then_inc(s_x, 16)
                    sp.dma_start(w1_sb[:, :, :], w1.rearrange("(h p) d -> p h d", p=P)).then_inc(s_w, 16)
                    sp.dma_start(w2_sb[:, :, :], w2.rearrange("(h p) d -> p h d", p=P)).then_inc(s_w, 16)
                    sp.dma_start(bias_sb[:, :], bias.rearrange("(o d) -> o d", o=1).to_broadcast([P, D])
                                 ).then_inc(s_w, 16)
                    for c in range(X_CHUNKS):
                        if c in LOW_ON_DVE:
                            sp.wait_ge(s_lo_dve, LOW_ON_DVE.index(c) + 1)
                        else:
                            sp.wait_ge(s_lo3, sum(i not in LOW_ON_DVE for i in range(c + 1)))
                        sp.dma_start(y_dram[c * BC * P:(c + 1) * BC * P, :].rearrange("(c p) d -> p c d", p=P),
                                     yp_1[:, c * BC:(c + 1) * BC, 0:PARTS * D]
                                     ).then_inc(s_ystore, 16)
                    sp.wait_ge(s_w, 48)

                @block.gpsimd
                def _(pool):
                    for k in range(2):
                        nc.gpsimd.memset(edge_i[:, k, FULL_CHUNKS:TC, :], PAD_ID)
                    nc.gpsimd.memset(xs[:, BLOCKS - 1, :], 0.0)
                    nc.gpsimd.memset(ident[:, :], 0.0)
                    nc.gpsimd.memset(ones[:, :], 1.0)
                    nc.gpsimd.memset(ones_b[:, :], 1.0)
                    nc.gpsimd.memset(zeros_b[:, :], 0.0)
                    nc.gpsimd.memset(ones_w[:, :], 1.0)
                    nc.gpsimd.memset(differ[:, :], 0.0)
                    nc.gpsimd.iota(thr_i[:, :], pattern=[[SET_N, SETS]], base=ND0, channel_multiplier=LIST_N)
                    nc.gpsimd.iota(held_i[0:1, :], pattern=[[P, GT // TILES // QUARTERS], [0, QUARTERS]], base=-LAG * P,
                                   channel_multiplier=0)
                    nc.gpsimd.iota(iota_i[:, :], pattern=[[1, LKEYS]], base=0, channel_multiplier=0)
                    nc.gpsimd.iota(start_i[:, :], pattern=[[LIST_N, P]], base=0, channel_multiplier=0)
                    nc.gpsimd.drain().then_inc(s_pad, 1)
                    pool.wait_ge(s_pad, 1)
                    nc.gpsimd.affine_select(out=ident[:, :], in_=ident[:, :], compare_op=ALU.not_equal, fill=1.0,
                                            base=0, pattern=[[-1, P]], channel_multiplier=1).then_inc(s_const, 1)
                    for at, (base, fill) in enumerate(((0, 0.5), (1, -0.5), (-(P - 1), 0.5))):
                        nc.gpsimd.affine_select(out=differ[:, :], in_=differ[:, :], compare_op=ALU.not_equal, fill=fill,
                                                base=base, pattern=[[-1, P]], channel_multiplier=1).then_inc(s_differ, 1)
                        pool.wait_ge(s_differ, at + 1)
                    nc.gpsimd.memset(wedge[:, :, :, :], PAD_ID).then_inc(s_wpad, 1)
                    pool.wait_ge(s_wpad, 1)
                    pool.wait_ge(s_widx, 1)
                    for s in range(SETS):
                        for r in range(WROWS):
                            for k, e in enumerate((src, dst)):
                                nc.gpsimd.indirect_dma_start(
                                    out=wedge[:, k, s, r * EROW:(r + 1) * EROW], out_offset=None,
                                    in_=e.rearrange("(r e) -> r e", e=EROW),
                                    in_offset=bass.IndirectOffsetOnAxis(ap=widx[:, s, r:r + 1], axis=0),
                                    bounds_check=E // EROW - 1, oob_is_err=False).then_inc(s_wrow, 16)
                    GE = GROUPS * TILES
                    m = [0]

                    def link(ins):
                        m[0] += 1
                        ins.then_inc(s_mask, 1)
                        pool.wait_ge(s_mask, m[0])

                    def within(mask, values, low, high):
                        link(nc.gpsimd.tensor_scalar(mask, values, low, high, ALU.max, ALU.min))
                        link(nc.gpsimd.tensor_tensor(mask, mask, values, ALU.subtract))
                        link(nc.gpsimd.tensor_scalar(mask, mask, 0.0, None, ALU.is_equal))

                    pool.wait_ge(s_near1, 1)
                    within(in_reach[:, :], near[0:1, 0:GROUPS], float(P), float(NEAR * P))
                    pool.wait_ge(s_rel, 1)
                    within(in_group[:, :], rel[:, 0:GE], 0.0, float(W - 1))
                    pool.wait_ge(s_wkey, 1)
                    within(in_window[:, :], wkey[:, 0, :, :].rearrange("p s e -> p (s e)"), 0.0, float(LKEYS - 1))
                    nc.gpsimd.memset(taken[:, GE + SETS * WE:], 0.0)
                    link(nc.gpsimd.tensor_copy(taken[:, GE:GE + SETS * WE], in_window[:, :]))
                    in_part = in_window[:, 0:GE]
                    link(nc.gpsimd.tensor_scalar(in_part, dstT[:, 0:GE], float(ND0), None, ALU.is_lt))
                    nc.gpsimd.tensor_tensor(taken[:, 0:GE], in_part, in_group[:, :], ALU.mult)
                    nc.gpsimd.tensor_copy(taken[0:1, GE + SETS * WE:], in_reach[:, :]).then_inc(s_masked, 1)
                    for c in range(X_CHUNKS):
                        if c not in LOW_ON_DVE:
                            pool.wait_ge(s_mid, c + 1)
                            b = slice(c * BC, (c + 1) * BC)
                            nc.gpsimd.tensor_tensor(yp[:, b, 2, :], xs[:, b, :], yp[:, b, 1, :],
                                                    ALU.subtract).then_inc(s_lo3, 1)

                @block.vector
                def _(dve):
                    n = [0]

                    def link(ins):
                        n[0] += 1
                        ins.then_inc(s_setup, 1)
                        dve.wait_ge(s_setup, n[0])

                    dve.wait_ge(s_pad, 1)
                    nc.vector.tensor_copy(iota_f[:, :], iota_i[:, 0:W])
                    nc.vector.tensor_copy(thr[:, :], thr_i[:, :])
                    nc.vector.tensor_copy(held[0:1, :], held_i[0:1, :])
                    nc.vector.tensor_copy(iota_h[:, :], iota_i[:, :])
                    nc.vector.tensor_copy(start_h[:, :], start_i[:, :])
                    link(nc.vector.tensor_copy(iota_b[:, :], iota_i[:, 0:P]))
                    dve.wait_ge(s_edges[1], 48)
                    nc.vector.tensor_copy(edge_f[:, 1, :, :], edge_i[:, 1, :, :]).then_inc(s_edgef, 1)
                    dve.wait_ge(s_edgef, 1)
                    row_starts = edge_f[:, 1, :, :].rearrange("p c (r e) -> p (c r) e", e=EROW)
                    link(nc.vector.tensor_scalar(row_i[:, :].unsqueeze(2), row_starts[:, :, 0:1], float(-ND0), None,
                                                 ALU.add))
                    nc.vector.tensor_single_scalar(row_bits[:, 0, :], row_i[:, :], SET_N.bit_length() - 1,
                                                   ALU.arith_shift_right)
                    link(nc.vector.tensor_single_scalar(row_bits[:, 1, :], row_i[:, :], SET_N - 1, ALU.bitwise_and))
                    link(nc.vector.tensor_copy(row_h[:, :, :], row_bits[:, :, :]))
                    for out_, op in ((in_set, ALU.is_equal), (before_set, ALU.is_gt)):
                        nc.vector.tensor_tensor(out_[:, :, :],
                                                iota_h[:, 0:SETS].unsqueeze(1).to_broadcast([P, ROW_CHUNKS, SETS]),
                                                row_h[:, 0, :].unsqueeze(2).to_broadcast([P, ROW_CHUNKS, SETS]), op)
                    SHARE = ROW_CHUNKS // 2
                    for c in range(0, ROW_CHUNKS, SHARE):
                        nc.vector.tensor_tensor(starts_below[:, c:c + SHARE, :],
                                                start_h[:, :].unsqueeze(1).to_broadcast([P, SHARE, P]),
                                                row_h[:, 1, c:c + SHARE].unsqueeze(2).to_broadcast([P, SHARE, P]),
                                                ALU.is_gt).then_inc(s_below, 1)
                    dve.wait_ge(s_trc, len(batches))
                    link(nc.vector.tensor_copy(srcT_i[:, :], srcT[:, :]))
                    dve.wait_ge(s_bcast, 1)
                    link(nc.vector.tensor_scalar(first[:, :], below_ps[:, 0:SETS], -1.0, 0.0, ALU.add, ALU.max))
                    nc.vector.tensor_tensor(widx[:, :, :], first[:, :].unsqueeze(2).to_broadcast([P, SETS, WROWS]),
                                            iota_f[:, 0:WROWS].unsqueeze(1).to_broadcast([P, SETS, WROWS]),
                                            ALU.add).then_inc(s_widx, 1)
                    nc.vector.tensor_single_scalar(bits[:, 0, :], srcT_i[:, :], P - 1, ALU.bitwise_and)
                    link(nc.vector.tensor_single_scalar(bits[:, 1, :], srcT_i[:, :], 7, ALU.arith_shift_right))
                    nc.vector.sem_inc(s_bits, 1)
                    link(nc.vector.tensor_copy(lohi[:, 1, :], bits[:, 1, :]))
                    dve.wait_ge(s_half, 1)
                    dve.wait_ge(s_iotax, 1)

                    def factor_hots(j, q):
                        g = j * UNROLL + q
                        for k, n, hots in ((1, BLOCKS, hi_hot1), (0, P, lo_hot1)):
                            if k == 0 and q in SIGN_GROUPS:
                                continue
                            dve.wait_ge(s_hist, g + (1 if k == 1 else HI_RING - 1))
                            half = q % HI_RING if k == 1 else sum(i not in SIGN_GROUPS for i in range(q)) % 2
                            last = nc.vector.tensor_tensor(hots[:, half, :, :], iota_x[:, 0:n, :],
                                                           lohi[:, k, bass.ds(g * HT, HT)].unsqueeze(1)
                                                           .to_broadcast([P, n, HT]), ALU.is_equal)
                        last.then_inc(s_hot1, 1)

                    with nc.vector.Fori(0, FIRST_TURNS) as j:
                        for q in range(UNROLL):
                            factor_hots(j, q)
                    nc.vector.tensor_scalar(idx_tab[:, :], srcT[:, 0:GT], float(N - 1), None, ALU.min)
                    dve.wait_ge(s_basep, 1)
                    link(nc.vector.tensor_tensor(near[0:1, :], base_ps[0:1, 0:GT // TILES], held[0:1, :], ALU.subtract))
                    nc.vector.sem_inc(s_near1, 1)
                    nc.vector.tensor_scalar(base_i[0:1, :], near[0:1, :], 0.0, float(NEAR * P), ALU.max, ALU.min)
                    nc.vector.tensor_tensor(rel[:, :].rearrange("p (g t) -> p g t", t=TILES),
                                            dstT[:, 0:GT].rearrange("p (g t) -> p g t", t=TILES),
                                            base_ps[:, 0:GT // TILES].unsqueeze(2)
                                            .to_broadcast([P, GT // TILES, TILES]), ALU.subtract).then_inc(s_rel, 1)
                    dve.wait_ge(s_wrow, 16 * SETS * WROWS * 2)
                    nc.vector.tensor_single_scalar(wbits[:, 0, :, :], wedge[:, 0, :, :], P - 1, ALU.bitwise_and)
                    nc.vector.tensor_single_scalar(wbits[:, 1, :, :], wedge[:, 0, :, :], 7, ALU.arith_shift_right)
                    for s in range(SETS):
                        last = nc.vector.tensor_scalar(wkey[:, 0, s, :], wedge[:, 1, s, :], thr[:, s:s + 1],
                                                       float(LIST_N), ALU.subtract, ALU.min)
                    link(last)
                    link(nc.vector.tensor_scalar(wkey[:, 0, :, :], wkey[:, 0, :, :], -1.0, float(BLOCKS),
                                                 ALU.max, ALU.mult))
                    nc.vector.tensor_copy(wkey[:, 1, :, :], wbits[:, 0, :, :])
                    nc.vector.tensor_tensor(wkey[:, 0, :, :], wkey[:, 0, :, :], wbits[:, 1, :, :],
                                            ALU.add).then_inc(s_wkey, 1)
                    with nc.vector.Fori(FIRST_TURNS, HIST_GROUPS // UNROLL) as j:
                        for q in range(UNROLL):
                            factor_hots(j, q)
                    dve.wait_ge(s_total, 1)
                    link(nc.vector.reduce_sum(total[0:1, :], total_ps[0:1, :], axis=AX_X))
                    nc.vector.tensor_scalar(general[0:1, :], total[0:1, :], float(E + GROUPS), None,
                                            ALU.not_equal).then_inc(s_flag, 1)
                    dve.wait_ge(s_histall, 1)
                    nc.vector.tensor_scalar(deg[:, :], hist_ps[:, 0:BLOCKS], 1.0, None, ALU.max).then_inc(s_deg, 1)
                    dve.wait_ge(s_sqrt, 1)
                    link(nc.vector.reciprocal(rs[:, :], rtmp[:, :]))
                    link(nc.vector.tensor_tensor(rtmp[:, :], rs[:, :], rs[:, :], ALU.mult))
                    link(nc.vector.tensor_tensor(rtmp[:, :], rtmp[:, :], deg[:, :], ALU.mult))
                    link(nc.vector.tensor_scalar(rtmp[:, :], rtmp[:, :], -0.5, 1.5, ALU.mult, ALU.add))
                    dve.wait_ge(s_x, 32)
                    nc.vector.tensor_tensor(rs[:, :], rs[:, :], rtmp[:, :], ALU.mult).then_inc(s_rs, 1)
                    dve.wait_ge(s_rs, 1)
                    for c in range(X_CHUNKS):
                        if c not in HIGH_ON_ACT:
                            for b in range(c * BC, (c + 1) * BC):
                                last = nc.vector.tensor_scalar(yp[:, b, 0, :], xs[:, b, :], rs[:, b:b + 1], None,
                                                               ALU.mult)
                            last.then_inc(s_hi, 1)
                            dve.wait_ge(s_hi, sum(i not in HIGH_ON_ACT for i in range(c + 1)))
                        else:
                            dve.wait_ge(s_hi_act, sum(i in HIGH_ON_ACT for i in range(c + 1)))
                        for b in range(c * BC, (c + 1) * BC):
                            last = nc.vector.scalar_tensor_tensor(out=xs[:, b, :], in0=xs[:, b, :],
                                                                  scalar=rs[:, b:b + 1], in1=yp[:, b, 0, :],
                                                                  op0=ALU.mult, op1=ALU.subtract)
                        last.then_inc(s_r1, 1)
                        if c in LOW_ON_DVE:
                            dve.wait_ge(s_mid, c + 1)
                            b = slice(c * BC, (c + 1) * BC)
                            nc.vector.tensor_tensor(yp[:, b, 2, :], xs[:, b, :], yp[:, b, 1, :],
                                                    ALU.subtract).then_inc(s_lo_dve, 1)

                @block.scalar
                def _(act):
                    act.wait_ge(s_edges[0], 48)
                    nc.scalar.copy(edge_f[:, 0, :, :], edge_i[:, 0, :, :]).then_inc(s_edgef_src, 1)
                    for b, (k, c, m) in enumerate(batches):
                        act.wait_ge(s_tr, b + 1)
                        nc.scalar.copy((srcT, dstT)[k][:, c * P:(c + m) * P], tr_ps[:, b % 2, 0:m * P]
                                       ).then_inc(s_trc, 1)
                    act.wait_ge(s_setup, 1)
                    nc.scalar.copy(iota_x[:, :, :], iota_b[:, :].unsqueeze(2).to_broadcast([P, P, HT])
                                   ).then_inc(s_iotax, 1)
                    act.wait_ge(s_bits, 1)
                    nc.scalar.copy(lohi[:, 0, :], bits[:, 0, :]).then_inc(s_half, 1)
                    nc.scalar.activation(half_lo[:, :], bits[:, 0, :], ACT.Copy, scale=-1.0, bias=0.5
                                         ).then_inc(s_half, 1)
                    act.wait_ge(s_half, 2)

                    def steps(j):
                        for at, q in enumerate(SIGN_GROUPS):
                            g = j * UNROLL + q
                            act.wait_ge(s_hist, g - (STEP_LEAD - HI_RING - 1))
                            for t in range(HT):
                                last = nc.scalar.activation(lo_step[:, at % 2, t, :], iota_b[:, :], ACT.Sign,
                                                            bias=half_lo[:, bass.ds(g * HT + t, 1)])
                            last.then_inc(s_step, 1)

                    with nc.scalar.Fori(0, FIRST_TURNS) as j:
                        steps(j)
                    for s in range(SETS):
                        for k in range(2):
                            b = 2 * s + k
                            act.wait_ge(s_wtr, b + 1)
                            tab = (key_tab, lo_tab)[k][:, s * P * LIST_T:(s + 1) * P * LIST_T]
                            nc.scalar.copy(tab.rearrange("p (w t) -> p t w", t=LIST_T),
                                           wt_ps[:, b % 2, 0:LIST_T * P].rearrange("p (t w) -> p t w", t=LIST_T)
                                           ).then_inc(s_wtc, 1)
                    with nc.scalar.Fori(FIRST_TURNS, HIST_GROUPS // UNROLL) as j:
                        steps(j)
                    act.wait_ge(s_steps, 1)
                    nc.scalar.copy(step_sums[:, :], step_ps[:, 0:BLOCKS]).then_inc(s_stepsum, 1)
                    act.wait_ge(s_deg, 1)
                    nc.scalar.activation(rtmp[:, :], deg[:, :], ACT.Sqrt).then_inc(s_sqrt, 1)
                    act.wait_ge(s_rs, 1)
                    for c in range(X_CHUNKS + 1):
                        if c in HIGH_ON_ACT:
                            for b in range(c * BC, (c + 1) * BC):
                                last = nc.scalar.activation(yp[:, b, 0, :], xs[:, b, :], ACT.Copy,
                                                            scale=rs[:, b:b + 1])
                            last.then_inc(s_hi_act, 1)
                        if c >= 1:
                            act.wait_ge(s_r1, c)
                            nc.scalar.copy(yp[:, (c - 1) * BC:c * BC, 1, :], xs[:, (c - 1) * BC:c * BC, :]
                                           ).then_inc(s_mid, 1)

                @block.tensor
                def _(pe):
                    pe.wait_ge(s_const, 1)
                    for b, (k, c, m) in enumerate(batches):
                        pe.wait_ge(s_edgef if k else s_edgef_src, 1)
                        if b >= 2:
                            pe.wait_ge(s_trc, b - 1)
                        for i in range(m):
                            last = nc.tensor.transpose(tr_ps[:, b % 2, i * P:(i + 1) * P],
                                                       edge_f[:, k, c + i, :], ident[:, :])
                        last.then_inc(s_tr, 1)
                    pe.wait_ge(s_trc, DST_BATCHES)
                    nc.tensor.matmul(base_ps[:, 0:GT // TILES], ones[0:1, :], dstT[0:1, 0:GT:TILES],
                                     start=True, stop=True).then_inc(s_basep, 1)
                    for c in range(ROW_CHUNKS):
                        pe.wait_ge(s_below, c // (ROW_CHUNKS // 2) + 1)
                        nc.tensor.matmul(below_ps[:, 0:SETS], starts_below[:, c, :], in_set[:, c, :],
                                         start=(c == 0), stop=False)
                        last = nc.tensor.matmul(below_ps[:, 0:SETS], ones_w[:, :], before_set[:, c, :],
                                                start=False, stop=(c == ROW_CHUNKS - 1))
                    last.then_inc(s_bcast, 1)
                    nc.tensor.matmul(hist_ps[:, 0:BLOCKS], zeros_b[:, :], zeros_b[:, 0:BLOCKS],
                                     start=True, stop=False)

                    nc.tensor.matmul(step_ps[:, 0:BLOCKS], zeros_b[:, :], zeros_b[:, 0:BLOCKS],
                                     start=True, stop=False)

                    def histogram(j, q):
                        g = j * UNROLL + q
                        pe.wait_ge(s_hot1, g + 1)
                        if q in SIGN_GROUPS:
                            at = SIGN_GROUPS.index(q)
                            pe.wait_ge(s_step, j * len(SIGN_GROUPS) + (at + 1))
                        half = sum(i not in SIGN_GROUPS for i in range(q)) % 2
                        for t in range(HT):
                            if q in SIGN_GROUPS:
                                last = nc.tensor.matmul(step_ps[:, 0:BLOCKS], lo_step[:, at % 2, t, :],
                                                        hi_hot1[:, q % HI_RING, :, t], start=False, stop=False)
                            else:
                                last = nc.tensor.matmul(hist_ps[:, 0:BLOCKS], lo_hot1[:, half, :, t],
                                                        hi_hot1[:, q % HI_RING, :, t], start=False, stop=False)
                        last.then_inc(s_hist, 1)

                    nc.tensor.sem_inc(s_hist, HI_RING)
                    with nc.tensor.Fori(0, FIRST_TURNS) as j:
                        for q in range(UNROLL):
                            histogram(j, q)
                    pe.wait_ge(s_wkey, 1)
                    for s in range(SETS):
                        for k in range(2):
                            b = 2 * s + k
                            if b >= 2:
                                pe.wait_ge(s_wtc, b - 1)
                            for t in range(LIST_T):
                                last = nc.tensor.transpose(wt_ps[:, b % 2, t * P:(t + 1) * P],
                                                           wkey[:, k, s, t * P:(t + 1) * P], ident[:, :])
                            last.then_inc(s_wtr, 1)
                    with nc.tensor.Fori(FIRST_TURNS, HIST_GROUPS // UNROLL) as j:
                        for q in range(UNROLL):
                            histogram(j, q)
                    nc.tensor.matmul(step_ps[:, 0:BLOCKS], zeros_b[:, :], zeros_b[:, 0:BLOCKS],
                                     start=False, stop=True).then_inc(s_steps, 1)
                    pe.wait_ge(s_masked, 1)
                    for at in range(0, TAKEN, 512):
                        n = min(512, TAKEN - at)
                        last = nc.tensor.matmul(total_ps[0:1, 0:n], ones_b[:, :], taken[:, at:at + n],
                                                start=(at == 0), stop=(at + n == TAKEN))
                    last.then_inc(s_total, 1)
                    pe.wait_ge(s_stepsum, 1)
                    pe.wait_ge(s_differ, 3)
                    nc.tensor.matmul(hist_ps[:, 0:BLOCKS], differ[:, :], step_sums[:, :],
                                     start=False, stop=True).then_inc(s_histall, 1)

        ph2 = ExitStack()
        with ph2:
            def sb2(name, shape, dt):
                return ph2.enter_context(nc.sbuf_tensor(name, shape, dt))

            def ps2(name, shape, dt=F32):
                return ph2.enter_context(nc.psum_tensor(name, shape, dt))

            y_rows = sb2("y_rows", [P, RING, TILES, PARTS * D], BF16)
            idx8 = sb2("idx8", [P, RING, TILES], I32)
            hot = sb2("hot", [P, 2, TILES, W], BF16)
            gT = sb2("gT", [P, 2 * H, NEAR * P + W], F32)
            cnt = sb2("cnt", [1, 2, NEAR * P + W], BF16)
            spread_lo = sb2("spread_lo", [P, WQ * WT, P], F16)
            lo_hot = sb2("lo_hot", [P, 2, WQ * WT, P], F16)
            key_hot = sb2("key_hot", [P, KEY_RING, WT, LKEYS], F16)
            counts = sb2("counts", [P, 2, BLOCKS, P], F16)
            zeros = sb2("zeros", [P, H, P], F32)
            gb = sb2("gb", [P, H, P], F32)
            cb = sb2("cb", [1, P], BF16)
            xb = sb2("xb", [P, 2, D], F32)
            has = sb2("has", [P, 2], F32)
            uv = sb2("uv", [P, 2, D], F32)
            uvT = sb2("uvT", [P, 2 * H, P], F32)
            emb = sb2("emb", [P, 2, D], F32)
            ysum = sb2("ysum", [P, 2, D], F32)
            o_sb = sb2("o_sb", [P, D], F32)
            ss = sb2("ss", [P, 2], F32)
            nrm = sb2("nrm", [P, 2], F32)
            inv = sb2("inv", [P, 2], F32)
            stats = sb2("stats", [P, 2, 6], F32)
            mv = sb2("mv", [P, 2, 2], F32)
            veps = sb2("veps", [P, 2], F32)
            std = sb2("std", [P, 2], F32)
            rstd = sb2("rstd", [P, 2], F32)
            grp_ps = ps2("grp_ps", [P, 2, 512])
            win_ps = ps2("win_ps", [P, 2, 512])
            g_ps = ps2("g_ps", [P, 2, 512])
            uvT_ps = ps2("uvT_ps", [P, 512])
            emb_ps = ps2("emb_ps", [P, 512])

            s_zero = sem("s_zero")
            s_idx = sem("s_idx")
            s_rows = [sem(f"s_rows{q}") for q in range(RING)]
            s_hot = sem("s_hot")
            s_grp = sem("s_grp")
            s_acc = sem("s_acc")
            s_spread = sem("s_spread")
            s_lo = sem("s_lo")
            s_key = sem("s_key")
            s_win = sem("s_win")
            s_cnt = sem("s_cnt")
            s_dense = sem("s_dense")
            s_gb = sem("s_gb")
            s_near = sem("s_near")
            s_g0 = sem("s_g0")

            def pair(name):
                return [sem(f"{name}0"), sem(f"{name}1")]

            s_xb = pair("s_xb"); s_uv = pair("s_uv"); s_uvT = pair("s_uvT"); s_uvc = pair("s_uvc")
            s_prod = pair("s_prod"); s_emb = pair("s_emb"); s_sq = pair("s_sq"); s_norm = pair("s_norm")
            s_v = pair("s_v"); s_var = pair("s_var"); s_std = pair("s_std"); s_o = pair("s_o")
            s_out = pair("s_out"); s_stored = pair("s_stored")

            CW = H * W
            STEPS = max(BG, BD - LEAD) + LAG
            LOOP = (LAG + 1, min(BG, BD - LEAD))
            SPLIT = [0] + [BLOCKS * i // (WB - 1) for i in range(WB)]

            def parts_of(j):
                if not isinstance(j, int):
                    return (QUARTERS, True, True, True, True)
                c = j + LEAD
                return (max(0, min(QUARTERS, GROUPS - j * QUARTERS)) if j >= 0 else 0, c < BD, 1 <= c <= BD,
                        LAG <= j < BG + LAG, LAG <= c < BD + LAG)

            def run(engine, step):
                for j in range(-LEAD, LOOP[0]):
                    step(j)
                with engine.Fori(*LOOP) as j:
                    step(j)
                for j in range(LOOP[1], STEPS):
                    step(j)

            def landed(j, q):
                return (j * (QUARTERS // RING) + (q // RING + 1)) * (16 * TILES)

            def turn(j, k):
                n = j - LAG + 1 - LEAD if k == 1 else j - LAG + 2 + LEAD
                return max(1, min(n, (BD, BG)[k] + 1)) if isinstance(j, int) else n

            def block_of(j, k):
                return j - LAG + k * BG

            with nc.Block() as block:
                @block.sync
                def _(sp):
                    def load(j, k):
                        b = block_of(j, k)
                        n = ROWS_LAST if isinstance(b, int) and b == BLOCKS - 1 else P
                        sp.dma_start(xb[0:n, k, :], x[bass.ds(b * P, n), :]).then_inc(s_xb[k], 16)

                    def finish(j, k, more):
                        b = block_of(j, k)
                        n = ROWS_LAST if isinstance(b, int) and b == BLOCKS - 1 else P
                        sp.wait_ge(s_o[k], j - LAG + 1)
                        sp.dma_start(out[bass.ds(b * P, n), :], o_sb[0:n, :]).then_inc(s_out[k], 16)
                        if more:
                            load(j + 1, k)
                        sp.wait_ge(s_out[k], (j - LAG) * 16 + 16)
                        sp.sem_inc(s_stored[k], 1)

                    def step(j):
                        for k in (1, 0):
                            if parts_of(j)[3 + k]:
                                finish(j + k * LEAD, k, not isinstance(j, int) or parts_of(j + 1)[3 + k])

                    def steps():
                        load(LAG, 1)
                        load(LAG, 0)
                        for k in range(2):
                            sp.sem_inc(s_stored[k], 1)
                        for j in range(LAG - LEAD, LAG):
                            step(j)
                        with nc.sync.Fori(LAG, LOOP[1]) as j:
                            step(j)
                        for j in range(LOOP[1], STEPS):
                            step(j)

                    steps()

                @block.gpsimd
                def _(pool):
                    def gathers(j, q):
                        pool.wait_ge(s_idx, j * QUARTERS + (q + 1))
                        nc.gpsimd.nop(nofuse=True)
                        pool.wait_ge(s_grp, j * QUARTERS + (q + 1))
                        nc.gpsimd.nop(nofuse=True)
                        for t in range(TILES):
                            nc.gpsimd.indirect_dma_start(
                                out=y_rows[:, q % RING, t, :], out_offset=None, in_=y_dram[:, :],
                                in_offset=bass.IndirectOffsetOnAxis(ap=idx8[:, q % RING, t:t + 1], axis=0)
                            ).then_inc(s_rows[q % RING], 16)

                    nc.gpsimd.memset(gT[:, :, :], 0.0)
                    nc.gpsimd.memset(zeros[:, :, :], 0.0)
                    nc.gpsimd.memset(cnt[:, :, :], 0.0)
                    nc.gpsimd.memset(yp_1[:, :, PARTS * D:], 1.0)
                    nc.gpsimd.drain().then_inc(s_zero, 1)
                    pool.wait_ge(s_ystore, 16 * X_CHUNKS)
                    nc.gpsimd.nop(nofuse=True)
                    with nc.gpsimd.Fori(0, GROUPS // QUARTERS) as j:
                        for q in range(QUARTERS):
                            gathers(j, q)
                    for g in range(GROUPS // QUARTERS * QUARTERS, GROUPS):
                        gathers(g // QUARTERS, g % QUARTERS)

                @block.scalar
                def _(act):
                    def copy_idx(j, q):
                        nc.scalar.copy(idx8[:, q % RING, :], idx_tab[:, bass.ds((j * QUARTERS + q) * TILES, TILES)]
                                       ).then_inc(s_idx, 1)

                    def spread(Q):
                        act.wait_ge(s_lo, Q + 1)
                        nc.scalar.copy(spread_lo[:, :, :],
                                       lo_tab[:, bass.ds(Q * (WQ * WT), WQ * WT)].unsqueeze(2)
                                       .to_broadcast([P, WQ * WT, P])).then_inc(s_spread, 1)

                    def keep_counts(j, i):
                        act.wait_ge(s_win, j * WB + (i + 3))
                        if i == 0:
                            act.wait_ge(s_dense, j + 1)
                        at = counts[:, bass.ds(j % 2, 1), :, i * WN:(i + 1) * WN].rearrange("p o s d -> p (o s) d")
                        nc.scalar.copy(at, win_ps[:, i % 2, 0:KEYS].rearrange("p (d s) -> p s d", s=BLOCKS)
                                       ).then_inc(s_cnt, 1)

                    def block_sums(j):
                        act.wait_ge(s_near, j)
                        act.wait_ge(s_g0, j - LAG + 1)
                        nc.scalar.copy(gb[:, :, :], gT[:, bass.ds((j % 2) * H, H), 0:P]).then_inc(s_gb, 1)
                        nc.scalar.copy(cb[0:1, :], cnt[0:1, bass.ds(j % 2, 1), 0:P].rearrange("p o n -> p (o n)")
                                       ).then_inc(s_gb, 1)

                    def copy_uvT(j, k):
                        act.wait_ge(s_uvT[k], j - LAG + 2)
                        act.wait_ge(s_prod[1 - k], turn(j, k))
                        nc.scalar.copy(uvT[:, :, :], uvT_ps[:, :].rearrange("p (h n) -> p h n", n=P)
                                       ).then_inc(s_uvc[k], 1)

                    def row_norm(j, k):
                        act.wait_ge(s_emb[k], j - LAG + 2)
                        nc.scalar.activation(ysum[:, k, :], emb[:, k, :], ACT.Square, accum_out=ss[:, k:k + 1]
                                             ).then_inc(s_sq[k], 1)
                        act.wait_ge(s_sq[k], j - LAG + 1)
                        nc.scalar.activation(nrm[:, k:k + 1], ss[:, k:k + 1], ACT.Sqrt).then_inc(s_norm[k], 1)

                    def row_std(j, k):
                        act.wait_ge(s_var[k], j - LAG + 1)
                        nc.scalar.activation(std[:, k:k + 1], veps[:, k:k + 1], ACT.Sqrt).then_inc(s_std[k], 1)

                    def step(j):
                        groups, windows, _, end0, end1 = parts_of(j)
                        c = j + LEAD
                        more = not isinstance(j, int) or c + 1 < BD
                        for q in range(QUARTERS):
                            for i in range(WQ):
                                if (q, i) == (2, 0) and end1:
                                    row_norm(c, 1)
                                if (q, i) == (2, 2) and end1:
                                    row_std(c, 1)
                                if (q, i) == (2, 3) and end0:
                                    row_norm(j, 0)
                                if (q, i) == (3, 1) and end0:
                                    row_std(j, 0)
                                if windows:
                                    keep_counts(c, q * WQ + i)
                                if (q, i) == (0, 1) and end0:
                                    block_sums(j)
                                if (q, i) == (0, 3) and end1:
                                    copy_uvT(c, 1)
                                if (q, i) == (1, 2) and end0:
                                    copy_uvT(j, 0)
                                if i == 1 and windows and (q < QUARTERS - 1 or more):
                                    spread(c * QUARTERS + (q + 2))
                            if not isinstance(j, int) or 0 <= j and j * QUARTERS + q + RING < GROUPS:
                                act.wait_ge(s_rows[q % RING], landed(j, q))
                                copy_idx(j, q + RING)

                    for q in range(RING):
                        copy_idx(0, q)
                    spread(0)
                    spread(1)
                    run(nc.scalar, step)

                @block.tensor
                def _(pe):
                    def group(j, q):
                        g = j * QUARTERS + q
                        pe.wait_ge(s_rows[q % RING], landed(j, q))
                        pe.wait_ge(s_hot, g + 1)
                        pe.wait_ge(s_acc, g + 1)
                        for h in range(H):
                            for t in range(TILES):
                                for m in range(PARTS):
                                    at = m * D + h * P
                                    nc.tensor.matmul(grp_ps[:, q % 2, h * W:(h + 1) * W], y_rows[:, q % RING, t, at:at + P],
                                                     hot[:, q % 2, t, :], start=(t == 0 and m == 0),
                                                     stop=(t == TILES - 1 and m == PARTS - 1))
                        for t in range(TILES):
                            last = nc.tensor.matmul(grp_ps[0:1, q % 2, CW:CW + W], ones_b[:, :], hot[:, q % 2, t, :],
                                                    start=(t == 0), stop=(t == TILES - 1))
                        last.then_inc(s_grp, 1)

                    def window(j, i):
                        if i % WQ == 0:
                            pe.wait_ge(s_lo, j * QUARTERS + (i // WQ + 2))
                        pe.wait_ge(s_key, j * WB + (i + 1))
                        pe.wait_ge(s_cnt, j * WB + (i + 1))
                        for t in range(WT):
                            at = t // LIST_T * LKEYS
                            last = nc.tensor.matmul(win_ps[:, i % 2, at:at + LKEYS],
                                                    lo_hot[:, (i // WQ) % 2, (i % WQ) * WT + t, :],
                                                    key_hot[:, i % KEY_RING, t, :],
                                                    start=(t % LIST_T == 0), stop=(t % LIST_T == LIST_T - 1))
                        last.then_inc(s_win, 1)

                    def product(j, i):
                        if i == 1:
                            if isinstance(j, int) and j == 1:
                                pe.wait_ge(s_zero, 1)
                            pe.wait_ge(s_cnt, j * WB + 2)
                            pe.wait_ge(s_uv[1], j)
                        for s in range(SPLIT[i], SPLIT[i + 1]):
                            lhsT = counts[:, bass.ds((j + 1) % 2, 1), s, :].rearrange("p o d -> p (o d)")
                            for m in range(PARTS) if s > 0 else reversed(range(PARTS)):
                                n = D + 1 if m == PARTS - 1 else D
                                last = nc.tensor.matmul(g_ps[:, 1, 0:n], lhsT, yp_1[:, s, m * D:m * D + n],
                                                        start=(s == 0 and m == PARTS - 1),
                                                        stop=(s == BLOCKS - 1 and m == PARTS - 1))
                        if i == WB - 1:
                            last.then_inc(s_dense, 1)

                    def turn_sums(j):
                        pe.wait_ge(s_gb, 2 * (j - LAG) + 2)
                        pe.wait_ge(s_uv[0], j - LAG + 1)
                        for h in range(H):
                            nc.tensor.transpose(g_ps[:, 0, h * P:(h + 1) * P], gb[:, h, :], ident[:, :])
                        nc.tensor.matmul(g_ps[:, 0, D:D + 1], cb[0:1, :], ones_b[0:1, 0:1],
                                         start=True, stop=True).then_inc(s_g0, 1)

                    def turn_uv(j, k):
                        pe.wait_ge(s_uv[k], j - LAG + 2)
                        pe.wait_ge(s_uvc[1 - k], turn(j, k))
                        for i in range(2):
                            for h in range(H):
                                last = nc.tensor.transpose(uvT_ps[:, (i * H + h) * P:(i * H + h + 1) * P],
                                                           uv[:, i, h * P:(h + 1) * P], ident[:, :])
                        last.then_inc(s_uvT[k], 1)

                    def weights(j, k):
                        pe.wait_ge(s_uvc[k], j - LAG + 2)
                        pe.wait_ge(s_emb[1 - k], turn(j, k))
                        for i, w in enumerate((w1_sb, w2_sb)):
                            for h in range(H):
                                last = nc.tensor.matmul(emb_ps[:, 0:D], uvT[:, i * H + h, :], w[:, h, :],
                                                        start=(i == 0 and h == 0), stop=(i == 1 and h == H - 1))
                        last.then_inc(s_prod[k], 1)

                    def step(j):
                        groups, windows, products, end0, end1 = parts_of(j)
                        c = j + LEAD
                        for q in range(QUARTERS):
                            if q < groups:
                                group(j, q)
                            for i in range(q * WQ, (q + 1) * WQ):
                                if windows:
                                    window(c, i)
                                if products:
                                    product(c, i)
                                if i == WQ - 1 and end0:
                                    turn_sums(j)
                                if i == 2 and end1:
                                    turn_uv(c, 1)
                                if i == WQ and end1:
                                    weights(c, 1)
                                if i == WQ + 1 and end0:
                                    turn_uv(j, 0)
                                if i == 2 * WQ - 1 and end0:
                                    weights(j, 0)

                    nc.tensor.sem_inc(s_grp, RING)
                    nc.tensor.sem_inc(s_win, 2)
                    nc.tensor.sem_inc(s_dense, 2)
                    nc.tensor.sem_inc(s_g0, 1)
                    for k in range(2):
                        nc.tensor.sem_inc(s_uvT[k], 1)
                        nc.tensor.sem_inc(s_prod[k], 1)
                    run(nc.tensor, step)

                @block.vector
                def _(dve):
                    def one_hots(j, q):
                        g = j * QUARTERS + q
                        dve.wait_ge(s_grp, g + (RING - 1))
                        nc.vector.tensor_tensor(hot[:, q % 2, :, :],
                                                iota_f[:, 0:W].unsqueeze(1).to_broadcast([P, TILES, W]),
                                                rel[:, bass.ds(g * TILES, TILES)].unsqueeze(2).to_broadcast([P, TILES, W]),
                                                ALU.is_equal).then_inc(s_hot, 1)

                    def accumulate(j, g, half):
                        if isinstance(g, int) and g == 0:
                            dve.wait_ge(s_zero, 1)
                        base = nc.vector.value_load(base_i[0:1, bass.ds(g, 1)], min_val=0, max_val=NEAR * P)
                        dve.wait_ge(s_grp, g + (RING + 1))
                        dve.wait_ge(s_acc, g + 2)
                        if not isinstance(j, int) or j > 0:
                            dve.wait_ge(s_near, j)
                        at = gT[:, bass.ds((j % 2) * H, H), bass.ds(base, W)]
                        nc.vector.tensor_tensor(at, at, grp_ps[:, half, 0:CW].rearrange("p (h w) -> p h w", h=H), ALU.add)
                        at = cnt[0:1, bass.ds(j % 2, 1), bass.ds(base, W)].rearrange("p o w -> p (o w)")
                        nc.vector.tensor_tensor(at, at, grp_ps[0:1, half, CW:CW + W], ALU.add).then_inc(s_acc, 1)

                    def move_on(j):
                        if not isinstance(j, int) or j > LAG:
                            dve.wait_ge(s_gb, 2 * (j - LAG))
                        dve.wait_ge(s_acc, (min(j * QUARTERS, GROUPS) if isinstance(j, int) else j * QUARTERS) + 2)
                        keep = (NEAR - 1) * P + W
                        new, old = bass.ds((j % 2) * H, H), bass.ds(((j + 1) % 2) * H, H)
                        nc.vector.tensor_copy(gT[:, new, 0:keep], gT[:, old, P:P + keep])
                        nc.vector.tensor_copy(gT[:, new, keep:], zeros[:, :, :])
                        new, old = bass.ds(j % 2, 1), bass.ds((j + 1) % 2, 1)
                        nc.vector.tensor_copy(cnt[0:1, new, 0:keep], cnt[0:1, old, P:P + keep])
                        nc.vector.tensor_copy(cnt[0:1, new, keep:], zeros[0:1, 0:1, :]).then_inc(s_near, 1)

                    def place_hots(Q, half):
                        dve.wait_ge(s_spread, Q + 1)
                        if not isinstance(Q, int) or Q > 1:
                            dve.wait_ge(s_win, Q * WQ - (WQ - 2))
                        nc.vector.tensor_tensor(lo_hot[:, half, :, :],
                                                iota_h[:, 0:P].unsqueeze(1).to_broadcast([P, WQ * WT, P]),
                                                spread_lo[:, :, :], ALU.is_equal).then_inc(s_lo, 1)

                    def key_hots(j, i):
                        if not isinstance(j, int) or j * WB + i >= KEY_RING:
                            dve.wait_ge(s_win, j * WB + (i + 3 - KEY_RING))
                        for t in range(WT):
                            last = nc.vector.tensor_scalar(key_hot[:, i % KEY_RING, t, :], iota_h[:, :],
                                                           key_tab[:, bass.ds((j * WB + i) * WT + t, 1)], None,
                                                           ALU.is_equal)
                        last.then_inc(s_key, 1)

                    def sums(j, k):
                        b = block_of(j, k)
                        if k == 0:
                            dve.wait_ge(s_g0, j - LAG + 2)
                        else:
                            dve.wait_ge(s_dense, j + 1)
                        dve.wait_ge(s_xb[k], (j - LAG) * 16 + 16)
                        dve.wait_ge(s_uvT[1 - k], turn(j, k))
                        nc.vector.tensor_scalar(has[:, k:k + 1], g_ps[:, k, D:D + 1], 0.0, None, ALU.is_gt)
                        nc.vector.scalar_tensor_tensor(out=uv[:, 0, :], in0=g_ps[:, k, 0:D],
                                                       scalar=rs[:, bass.ds(b, 1)], in1=xb[:, k, :],
                                                       op0=ALU.mult, op1=ALU.add)
                        nc.vector.scalar_tensor_tensor(out=uv[:, 1, :], in0=g_ps[:, k, 0:D],
                                                       scalar=rs[:, bass.ds(b, 1)], in1=xb[:, k, :],
                                                       op0=ALU.mult, op1=ALU.mult).then_inc(s_uv[k], 1)

                    LINKS = 8

                    def link(ins, j, k, at):
                        ins.then_inc(s_v[k], 1)
                        dve.wait_ge(s_v[k], (j - LAG) * LINKS + at)

                    def embed(j, k):
                        dve.wait_ge(s_prod[k], j - LAG + 2)
                        link(nc.vector.scalar_tensor_tensor(out=emb[:, k, :], in0=emb_ps[:, 0:D], scalar=has[:, k:k + 1],
                                                            in1=bias_sb[:, :], op0=ALU.mult, op1=ALU.add), j, k, 1)
                        nc.vector.scalar_tensor_tensor(out=emb[:, k, :], in0=emb[:, k, :], scalar=0.01,
                                                       in1=emb[:, k, :], op0=ALU.mult, op1=ALU.max).then_inc(s_emb[k], 1)

                    def residual(j, k):
                        dve.wait_ge(s_norm[k], j - LAG + 1)
                        link(nc.vector.tensor_scalar(nrm[:, k:k + 1], nrm[:, k:k + 1], 1e-12, None, ALU.max), j, k, 2)
                        link(nc.vector.reciprocal(inv[:, k:k + 1], nrm[:, k:k + 1]), j, k, 3)
                        link(nc.vector.scalar_tensor_tensor(out=ysum[:, k, :], in0=emb[:, k, :], scalar=inv[:, k:k + 1],
                                                            in1=xb[:, k, :], op0=ALU.mult, op1=ALU.add), j, k, 4)
                        link(nc.vector.bn_stats(stats[:, k, :], ysum[:, k, :]), j, k, 5)
                        nc.vector.nop(nofuse=True)
                        link(nc.vector.bn_aggr(mv[:, k, :], stats[:, k, :]), j, k, 6)
                        nc.vector.tensor_scalar(veps[:, k:k + 1], mv[:, k, 1:2], 1e-5, None, ALU.add).then_inc(s_var[k], 1)

                    def layer_norm(j, k):
                        dve.wait_ge(s_std[k], j - LAG + 1)
                        link(nc.vector.reciprocal(rstd[:, k:k + 1], std[:, k:k + 1]), j, k, 7)
                        dve.wait_ge(s_stored[1 - k], turn(j, k))
                        nc.vector.tensor_scalar(o_sb[:, :], ysum[:, k, :], mv[:, k, 0:1], rstd[:, k:k + 1],
                                                ALU.subtract, ALU.mult).then_inc(s_o[k], 1)
                        nc.vector.sem_inc(s_v[k], 1)

                    def step(j):
                        groups, windows, _, end0, end1 = parts_of(j)
                        c = j + LEAD
                        for q in range(QUARTERS):
                            i = q * WQ
                            if windows:
                                key_hots(c, i)
                            if q < groups:
                                one_hots(j, q + 1)
                            if q == 1 and end0:
                                sums(j, 0)
                            if windows:
                                key_hots(c, i + 1)
                            if q == 0 and end1:
                                sums(c, 1)
                            if q == 3 and end1:
                                layer_norm(c, 1)
                            if q == 3 and end0:
                                residual(j, 0)
                            if windows:
                                key_hots(c, i + 2)
                            if windows and (q < QUARTERS - 1 or not isinstance(j, int) or c + 1 < BD):
                                place_hots(c * QUARTERS + (q + 1), (q + 1) % 2)
                            if not isinstance(j, int) or 0 < j * QUARTERS + q <= GROUPS:
                                accumulate(j - 1 if q == 0 else j, j * QUARTERS + q - 1, (q + 1) % 2)
                            if q == 2 and end1:
                                residual(c, 1)
                            if q == 2 and end0:
                                embed(j, 0)
                            if windows:
                                key_hots(c, i + 3)
                            if q == 0 and (not isinstance(j, int) or 0 < j < BG + LAG):
                                move_on(j)
                            if q == 1 and end1:
                                embed(c, 1)
                            if q == 3 and end0:
                                layer_norm(j, 0)

                    nc.vector.sem_inc(s_acc, 2)
                    nc.vector.sem_inc(s_lo, 1)
                    nc.vector.sem_inc(s_cnt, 2)
                    for k in range(2):
                        nc.vector.sem_inc(s_uv[k], 1)
                        nc.vector.sem_inc(s_uvc[k], 1)
                        nc.vector.sem_inc(s_emb[k], 1)
                    one_hots(0, 0)
                    place_hots(0, 0)
                    run(nc.vector, step)


        ph3 = ExitStack()
        with ph3:
            def sb3(name, shape, dt):
                return ph3.enter_context(nc.sbuf_tensor(name, shape, dt))

            def ps3(name, shape):
                return ph3.enter_context(nc.psum_tensor(name, shape, F32))

            PASSES = BLOCKS // SPAN
            NODES = SPAN * P
            LISTS = next(n for n in range(P, 0, -1) if E % n == 0 and E // n % (SLOTS * BATCH) == 0)
            EDGES = E // LISTS
            TURNS = EDGES // (SLOTS * BATCH)
            LINKS3 = 8
            assert PASSES * SPAN == BLOCKS

            p_src = sb3("p_src", [P, EDGES], I32)
            p_dsti = sb3("p_dsti", [P, EDGES], I32)
            p_dst = sb3("p_dst", [P, EDGES], F32)
            p_iotai = sb3("p_iotai", [P, NODES], I32)
            p_iota = sb3("p_iota", [P, NODES], F16)
            p_zeros = sb3("p_zeros", [P, D + 1], BF16)
            p_rownum = sb3("p_rownum", [P, SLOTS, BATCH], I32)
            p_rows = sb3("p_rows", [P, SLOTS, BATCH, PARTS * D], BF16)
            p_hot = sb3("p_hot", [P, 2, BATCH, NODES], F16)
            p_x = sb3("p_x", [P, D], F32)
            p_has = sb3("p_has", [P, 1], F32)
            p_uv = sb3("p_uv", [P, 2, D], F32)
            p_uvT = sb3("p_uvT", [P, 2 * H, P], F32)
            p_emb = sb3("p_emb", [P, D], F32)
            p_y = sb3("p_y", [P, D], F32)
            p_out = sb3("p_out", [P, D], F32)
            p_ss = sb3("p_ss", [P, 1], F32)
            p_norm = sb3("p_norm", [P, 1], F32)
            p_inv = sb3("p_inv", [P, 1], F32)
            p_stats = sb3("p_stats", [P, 6], F32)
            p_mv = sb3("p_mv", [P, 2], F32)
            p_veps = sb3("p_veps", [P, 1], F32)
            p_std = sb3("p_std", [P, 1], F32)
            p_rstd = sb3("p_rstd", [P, 1], F32)
            sum_ps = ps3("sum_ps", [P, SPAN, 512])
            turn_ps = ps3("turn_ps", [P, 512])

            q_pad = sem("q_pad"); q_edges = sem("q_edges"); q_iota = sem("q_iota"); q_setup = sem("q_setup")
            q_zeros = sem("q_zeros")
            q_num = sem("q_num")
            q_rows = [sem(f"q_rows{b}") for b in range(SLOTS)]
            q_hot = sem("q_hot")
            q_batch = sem("q_batch")
            q_move = sem("q_move")
            q_sums = sem("q_sums")
            q_x = sem("q_x"); q_uv = sem("q_uv"); q_turned = sem("q_turned"); q_uvT = sem("q_uvT")
            q_prod = sem("q_prod"); q_emb = sem("q_emb"); q_sq = sem("q_sq"); q_norm = sem("q_norm")
            q_v = sem("q_v"); q_var = sem("q_var"); q_std = sem("q_std"); q_out = sem("q_out")
            q_done = sem("q_done"); q_stored = sem("q_stored")

            def run_passes(engine, one_pass):
                with engine.Fori(0, PASSES - 1) as p:
                    one_pass(p)
                one_pass(PASSES - 1)

            def run_batches(engine, p, batch):
                with engine.Fori(0, TURNS) as t:
                    for b in range(SLOTS):
                        batch(p * TURNS + t, (p * TURNS + t) * SLOTS + b, b, t)

            def rows_of(p, i):
                return ROWS_LAST if isinstance(p, int) and p * SPAN + i == BLOCKS - 1 else P

            def when_general(engine):
                flag = engine.value_load(general[0:1, 0:1], min_val=0, max_val=1)
                return engine.If(flag > 0)

            with nc.Block() as block:
                @block.sync
                def _(sp):
                    with when_general(nc.sync):
                        sp.wait_ge(q_pad, 1)
                        sp.dma_start(p_src[0:LISTS, :], src.rearrange("(q e) -> q e", e=EDGES)).then_inc(q_edges, 16)
                        sp.dma_start(p_dsti[0:LISTS, :], dst.rearrange("(q e) -> q e", e=EDGES)).then_inc(q_edges, 16)
                        sp.wait_ge(q_edges, 32)

                        def stores(p):
                            for i in range(SPAN):
                                at = p * (SPAN * P) + i * P
                                n = rows_of(p, i)
                                sp.dma_start(p_x[0:n, :], x[bass.ds(at, n), :]).then_inc(q_x, 16)
                                sp.wait_ge(q_out, p * SPAN + (i + 1))
                                sp.dma_start(out[bass.ds(at, n), :], p_out[0:n, :]).then_inc(q_done, 16)
                                sp.wait_ge(q_done, (p * SPAN + (i + 1)) * 16)
                                sp.sem_inc(q_stored, 1)

                        sp.sem_inc(q_stored, 1)
                        run_passes(nc.sync, stores)

                @block.gpsimd
                def _(pool):
                    with when_general(nc.gpsimd):
                        nc.gpsimd.memset(p_src[:, :], 0)
                        nc.gpsimd.memset(p_dsti[:, :], PAD_ID)
                        nc.gpsimd.memset(p_x[:, :], 0.0)
                        nc.gpsimd.drain().then_inc(q_pad, 1)
                        nc.gpsimd.iota(p_iotai[:, :], pattern=[[1, NODES]], base=0,
                                       channel_multiplier=0).then_inc(q_iota, 1)

                        def gathers(turn, n, slot, t):
                            pool.wait_ge(q_num, n + 1)
                            nc.gpsimd.nop(nofuse=True)
                            pool.wait_ge(q_batch, n + 1)
                            nc.gpsimd.nop(nofuse=True)
                            for k in range(BATCH):
                                nc.gpsimd.indirect_dma_start(
                                    out=p_rows[:, slot, k, :], out_offset=None, in_=y_dram[:, :],
                                    in_offset=bass.IndirectOffsetOnAxis(ap=p_rownum[:, slot, k:k + 1], axis=0)
                                ).then_inc(q_rows[slot], 16)

                        run_passes(nc.gpsimd, lambda p: run_batches(nc.gpsimd, p, gathers))

                @block.scalar
                def _(act):
                    with when_general(nc.scalar):
                        act.wait_ge(q_edges, 32)

                        def numbers(turn, n, slot, t):
                            act.wait_ge(q_batch, n + 1)
                            nc.scalar.copy(p_rownum[:, slot, :],
                                           p_src[:, bass.ds(t * (SLOTS * BATCH) + slot * BATCH, BATCH)]
                                           ).then_inc(q_num, 1)

                        def ends(p):
                            run_batches(nc.scalar, p, numbers)
                            for i in range(SPAN):
                                n = p * SPAN + i
                                act.wait_ge(q_turned, n + 1)
                                nc.scalar.copy(p_uvT[:, :, :], turn_ps[:, :].rearrange("p (h n) -> p h n", n=P)
                                               ).then_inc(q_uvT, 1)
                                act.wait_ge(q_emb, n + 2)
                                nc.scalar.activation(p_y[:, :], p_emb[:, :], ACT.Square, accum_out=p_ss[:, :]
                                                     ).then_inc(q_sq, 1)
                                act.wait_ge(q_sq, n + 1)
                                nc.scalar.activation(p_norm[:, :], p_ss[:, :], ACT.Sqrt).then_inc(q_norm, 1)
                                act.wait_ge(q_var, n + 1)
                                nc.scalar.activation(p_std[:, :], p_veps[:, :], ACT.Sqrt).then_inc(q_std, 1)

                        run_passes(nc.scalar, ends)

                @block.tensor
                def _(pe):
                    with when_general(nc.tensor):
                        def batch(turn, n, slot, t):
                            pe.wait_ge(q_rows[slot], turn * (16 * BATCH) + 16 * BATCH)
                            pe.wait_ge(q_hot, n + 1)
                            for k in range(BATCH):
                                for i in range(SPAN):
                                    lhsT = p_hot[:, slot % 2, k, i * P:(i + 1) * P]
                                    for m in range(PARTS):
                                        nc.tensor.matmul(sum_ps[:, i, 0:D], lhsT, p_rows[:, slot, k, m * D:(m + 1) * D],
                                                         start=False, stop=False, skip_group_check=True)
                                    last = nc.tensor.matmul(sum_ps[:, i, D:D + 1], lhsT, ones_b[:, :],
                                                            start=False, stop=False, skip_group_check=True)
                            last.then_inc(q_batch, 1)

                        def blocks(p):
                            pe.wait_ge(q_emb, p * SPAN + 1)
                            for i in range(SPAN):
                                nc.tensor.matmul(sum_ps[:, i, 0:D + 1], p_zeros[:, 0:P], p_zeros[:, :],
                                                 start=True, stop=False, skip_group_check=True)
                            run_batches(nc.tensor, p, batch)
                            for i in range(SPAN):
                                last = nc.tensor.matmul(sum_ps[:, i, 0:D + 1], p_zeros[:, 0:P], p_zeros[:, :],
                                                        start=False, stop=True, skip_group_check=True)
                            last.then_inc(q_sums, 1)
                            for i in range(SPAN):
                                n = p * SPAN + i
                                pe.wait_ge(q_uv, n + 1)
                                for a in range(2):
                                    for h in range(H):
                                        last = nc.tensor.transpose(turn_ps[:, (a * H + h) * P:(a * H + h + 1) * P],
                                                                   p_uv[:, a, h * P:(h + 1) * P], ident[:, :])
                                last.then_inc(q_turned, 1)
                                pe.wait_ge(q_uvT, n + 1)
                                for a, w in enumerate((w1_sb, w2_sb)):
                                    for h in range(H):
                                        last = nc.tensor.matmul(sum_ps[:, i, 0:D], p_uvT[:, a * H + h, :], w[:, h, :],
                                                                start=(a == 0 and h == 0), stop=(a == 1 and h == H - 1))
                                last.then_inc(q_prod, 1)

                        nc.tensor.sem_inc(q_batch, SLOTS)
                        pe.wait_ge(q_zeros, 1)
                        run_passes(nc.tensor, blocks)

                @block.vector
                def _(dve):
                    with when_general(nc.vector):
                        def one_hots(turn, n, slot, t):
                            dve.wait_ge(q_batch, n + (SLOTS - 1))
                            for k in range(BATCH):
                                last = nc.vector.tensor_scalar(
                                    p_hot[:, slot % 2, k, :], p_iota[:, :],
                                    p_dst[:, bass.ds(t * (SLOTS * BATCH) + (slot * BATCH + k), 1)], None, ALU.is_equal)
                            last.then_inc(q_hot, 1)

                        def link(ins, n, at):
                            ins.then_inc(q_v, 1)
                            dve.wait_ge(q_v, n * LINKS3 + at)

                        def ends(p):
                            run_batches(nc.vector, p, one_hots)
                            dve.wait_ge(q_sums, p + 1)
                            for i in range(SPAN):
                                n = p * SPAN + i
                                dve.wait_ge(q_x, n * 16 + 16)
                                nc.vector.tensor_scalar(p_has[:, :], sum_ps[:, i, D:D + 1], 0.0, None, ALU.is_gt)
                                for a, op in enumerate((ALU.add, ALU.mult)):
                                    last = nc.vector.scalar_tensor_tensor(
                                        out=p_uv[:, a, :], in0=sum_ps[:, i, 0:D], scalar=rs[:, bass.ds(n, 1)],
                                        in1=p_x[:, :], op0=ALU.mult, op1=op)
                                last.then_inc(q_uv, 1)
                                dve.wait_ge(q_prod, n + 1)
                                link(nc.vector.scalar_tensor_tensor(
                                    out=p_emb[:, :], in0=sum_ps[:, i, 0:D], scalar=p_has[:, :], in1=bias_sb[:, :],
                                    op0=ALU.mult, op1=ALU.add), n, 1)
                                nc.vector.scalar_tensor_tensor(
                                    out=p_emb[:, :], in0=p_emb[:, :], scalar=0.01, in1=p_emb[:, :],
                                    op0=ALU.mult, op1=ALU.max).then_inc(q_emb, 1)
                                dve.wait_ge(q_norm, n + 1)
                                link(nc.vector.tensor_scalar(p_norm[:, :], p_norm[:, :], 1e-12, None, ALU.max), n, 2)
                                link(nc.vector.reciprocal(p_inv[:, :], p_norm[:, :]), n, 3)
                                link(nc.vector.scalar_tensor_tensor(
                                    out=p_y[:, :], in0=p_emb[:, :], scalar=p_inv[:, :], in1=p_x[:, :],
                                    op0=ALU.mult, op1=ALU.add), n, 4)
                                link(nc.vector.bn_stats(p_stats[:, :], p_y[:, :]), n, 5)
                                nc.vector.nop(nofuse=True)
                                link(nc.vector.bn_aggr(p_mv[:, :], p_stats[:, :]), n, 6)
                                nc.vector.tensor_scalar(p_veps[:, :], p_mv[:, 1:2], 1e-5, None,
                                                        ALU.add).then_inc(q_var, 1)
                                dve.wait_ge(q_std, n + 1)
                                link(nc.vector.reciprocal(p_rstd[:, :], p_std[:, :]), n, 7)
                                dve.wait_ge(q_stored, n + 1)
                                nc.vector.tensor_scalar(p_out[:, :], p_y[:, :], p_mv[:, 0:1], p_rstd[:, :],
                                                        ALU.subtract, ALU.mult).then_inc(q_out, 1)
                                nc.vector.sem_inc(q_v, 1)
                            nc.vector.tensor_scalar(p_dst[:, :], p_dst[:, :], float(NODES), None,
                                                    ALU.subtract).then_inc(q_move, 1)
                            dve.wait_ge(q_move, p + 1)

                        nc.vector.memset(p_zeros[:, :], 0.0).then_inc(q_zeros, 1)
                        nc.vector.sem_inc(q_emb, 1)
                        dve.wait_ge(q_iota, 1)
                        nc.vector.tensor_copy(p_iota[:, :], p_iotai[:, :])
                        dve.wait_ge(q_edges, 32)
                        nc.vector.tensor_copy(p_dst[:, :], p_dsti[:, :]).then_inc(q_setup, 1)
                        dve.wait_ge(q_setup, 1)
                        run_passes(nc.vector, ends)


_INS = ['x', 'src', 'dst', 'L0_gnn_W1', 'L0_gnn_W2', 'L0_gnn_b']


def kernel(**inputs):
    import numpy as _np
    import concourse.bacc as _bacc
    from concourse import mybir as _mybir
    from concourse.bass_utils import run_bass_kernel_spmd as _run

    nc = _bacc.Bacc("TRN2", target_bir_lowering=False, num_devices=1)
    arrays, args = {}, []
    for name in _INS:
        a = _np.ascontiguousarray(inputs[name])
        arrays[f"in_{name}_dram"] = a
        args.append(nc.dram_tensor(f"in_{name}_dram", a.shape, _mybir.dt.from_np(a.dtype), kind="ExternalInput").ap())
    shape = tuple(inputs['x'].shape)
    args.append(nc.dram_tensor("out_0_dram", shape, _mybir.dt.float32, kind="ExternalOutput").ap())
    build(nc, *args)
    r = _run(nc, [arrays], core_ids=[0])
    return r.results[0]["out_0_dram"]
```
